# Optimizing a Trainium2 kernel written in Bass

```python
import numpy as np
import jax
import jax.numpy as jnp

def _softmax(x, axis=-1):
    return jax.nn.softmax(x, axis=axis)

def _gelu(x):
    return jax.nn.gelu(x, approximate=True)

def _silu(x):
    return jax.nn.silu(x)

def _sigmoid(x):
    return jax.nn.sigmoid(x)

def _layernorm(x, axis=-1, eps=1e-05):
    m = jnp.mean(x, axis=axis, keepdims=True)
    v = jnp.var(x, axis=axis, keepdims=True)
    return (x - m) / jnp.sqrt(v + eps)

def _scatter_add(tgt, idx, src, axis=0):
    return tgt.at[idx].add(src)

def _segment_sum(src, seg, n):
    return jax.ops.segment_sum(src, seg, n)
kernel_name = 'mk_gnn_preln_d2_gnn_r32_c9fb07'

def setup_inputs(seed: int=0):
    np.random.seed(seed)
    _w = jnp.asarray

    def _rec_inputs():
        import jax
        import jax.numpy as jnp
        _gk = jax.random.key(seed)
        x = -0.000202 + 1 * jax.random.normal(jax.random.fold_in(_gk, 1), (50000, 128), jnp.float32)
        src = jax.random.randint(jax.random.fold_in(_gk, 2), (50000,), 0, 50000, jnp.int32)
        dst = jax.random.randint(jax.random.fold_in(_gk, 3), (50000,), 0, 50000, jnp.int32)
        _o = jnp.argsort(dst, stable=True)
        src = src[_o]
        dst = dst[_o]
        edge_attr_2 = -0.000414295 + 0.999828 * jax.random.normal(jax.random.fold_in(_gk, 12), (50000, 2), jnp.float32)
        edge_weight = jax.random.uniform(jax.random.fold_in(_gk, 14), (50000,), jnp.float32, 0.0, 0.999998)
        return (x, src, dst, edge_attr_2, edge_weight)
    x, src, dst, edge_attr_2, edge_weight = _rec_inputs()

    def _L0_gnn_setup():
        import jax, jax.numpy as jnp
        import numpy as np
        MIN_NORM = 1e-15
        EPS_BALL = 0.004
        ARCTANH_CLIP = 1.0 - 1e-07
        C = 1.0

        def _norm(x):
            return jnp.clip(jnp.linalg.norm(x, axis=-1, keepdims=True), MIN_NORM, None)

        def proj(x, c=C):
            maxnorm = (1.0 - EPS_BALL) / jnp.sqrt(c)
            n = _norm(x)
            return jnp.where(n > maxnorm, x / n * maxnorm, x)

        def expmap0(u, c=C):
            sc = jnp.sqrt(c)
            n = _norm(u)
            return jnp.tanh(sc * n) * u / (sc * n)

        def logmap0(p, c=C):
            sc = jnp.sqrt(c)
            n = _norm(p)
            return jnp.arctanh(jnp.clip(sc * n, None, ARCTANH_CLIP)) * p / (sc * n)

        def mobius_add(x, y, c=C):
            x2 = jnp.sum(x * x, -1, keepdims=True)
            y2 = jnp.sum(y * y, -1, keepdims=True)
            xy = jnp.sum(x * y, -1, keepdims=True)
            num = (1.0 + 2.0 * c * xy + c * y2) * x + (1.0 - c * x2) * y
            den = 1.0 + 2.0 * c * xy + c * c * x2 * y2
            return num / jnp.clip(den, MIN_NORM, None)

        def mobius_matvec(W, x, c=C):
            sc = jnp.sqrt(c)
            xn = _norm(x)
            mx = x @ W.T
            mxn = _norm(mx)
            res = jnp.tanh(mxn / xn * jnp.arctanh(jnp.clip(sc * xn, None, ARCTANH_CLIP))) * mx / (mxn * sc)
            zero = jnp.all(mx == 0, axis=-1, keepdims=True)
            return jnp.where(zero, 0.0, res)

        def hyp_linear(x, W, b, c=C):
            mv = proj(mobius_matvec(W, x, c), c)
            bias = proj(expmap0(b[None, :], c), c)
            return proj(mobius_add(mv, bias, c), c)

        def hyp_agg(x, src, dst, w, n_nodes, c=C):
            xt = logmap0(x, c)
            msg = w[:, None] * xt[src]
            agg = jax.ops.segment_sum(msg, dst, num_segments=n_nodes)
            return proj(expmap0(agg, c), c)

        def hyp_act(x, c_in=C, c_out=C):
            xt = jax.nn.relu(logmap0(x, c_in))
            return proj(expmap0(xt, c_out), c_out)

        def hgcn_conv(x, src, dst, w, W, b, c_in=C, c_out=C):
            h = hyp_linear(x, W, b, c_in)
            h = hyp_agg(h, src, dst, w, x.shape[0], c_in)
            return hyp_act(h, c_in, c_out)
        key = jax.random.key(seed)
        ks = jax.random.split(key, 7)
        N, E, D_IN, D_H = (50000, 25000, 128, 128)
        x = jax.random.normal(ks[0], (N, D_IN), dtype=jnp.float32)
        edge_index = jax.random.randint(ks[1], (2, E), 0, N, dtype=jnp.int32)
        edge_weight = jax.random.uniform(ks[2], (E,), dtype=jnp.float32)
        W1 = jax.random.normal(ks[3], (D_H, D_IN), dtype=jnp.float32) * 0.1
        b1 = jax.random.normal(ks[4], (D_H,), dtype=jnp.float32) * 0.1
        W2 = jax.random.normal(ks[5], (D_H, D_H), dtype=jnp.float32) * 0.1
        b2 = jax.random.normal(ks[6], (D_H,), dtype=jnp.float32) * 0.1
        return {'x': x, 'edge_index': edge_index, 'edge_weight': edge_weight, 'W1': W1, 'b1': b1, 'W2': W2, 'b2': b2}
    _L0_gnn_all = _L0_gnn_setup()
    _L0_gnn_in = {k: v for k, v in _L0_gnn_all.items() if k in ('W1', 'b1', 'W2', 'b2')}
    del _L0_gnn_all

    def _L1_gnn_setup():
        import jax, jax.numpy as jnp
        import numpy as np
        N_NODES = 50000
        N_EDGES = 25000
        IN_DIM = 128
        P = 2
        OUT_DIM = 128
        key = jax.random.key(seed)
        k1, k2, k3, k4, k5, k6 = jax.random.split(key, 6)
        features = jax.random.normal(k1, (N_NODES, IN_DIM), dtype=jnp.float32)
        edge_inputs = jax.random.normal(k2, (N_EDGES, P), dtype=jnp.float32)
        scale = 1.0 / np.sqrt(P * IN_DIM)
        W = jax.random.uniform(k3, (OUT_DIM, P * IN_DIM), dtype=jnp.float32, minval=-scale, maxval=scale)
        b = jax.random.uniform(k4, (OUT_DIM,), dtype=jnp.float32, minval=-scale, maxval=scale)
        src = jax.random.randint(k5, (N_EDGES,), 0, N_NODES, dtype=jnp.int32)
        dst = jax.random.randint(k6, (N_EDGES,), 0, N_NODES, dtype=jnp.int32)
        return {'features': features, 'edge_inputs': edge_inputs, 'W': W, 'b': b, 'src': src, 'dst': dst}
    _L1_gnn_all = _L1_gnn_setup()
    _L1_gnn_in = {k: v for k, v in _L1_gnn_all.items() if k in ('W', 'b')}
    del _L1_gnn_all
    return {'x': x, 'src': src, 'dst': dst, 'edge_attr_2': edge_attr_2, 'edge_weight': edge_weight, 'L0_gnn_W1': _L0_gnn_in['W1'], 'L0_gnn_b1': _L0_gnn_in['b1'], 'L0_gnn_W2': _L0_gnn_in['W2'], 'L0_gnn_b2': _L0_gnn_in['b2'], 'L1_gnn_W': _L1_gnn_in['W'], 'L1_gnn_b': _L1_gnn_in['b']}

def reference(x, src, dst, edge_attr_2, edge_weight, L0_gnn_W1, L0_gnn_b1, L0_gnn_W2, L0_gnn_b2, L1_gnn_W, L1_gnn_b):
    import jax
    import jax.numpy as jnp

    def _L0_gnn_ref(x, edge_index, edge_weight, W1, b1, W2, b2):
        import jax, jax.numpy as jnp
        import numpy as np
        MIN_NORM = 1e-15
        EPS_BALL = 0.004
        ARCTANH_CLIP = 1.0 - 1e-07
        C = 1.0

        def _norm(x):
            return jnp.clip(jnp.linalg.norm(x, axis=-1, keepdims=True), MIN_NORM, None)

        def proj(x, c=C):
            maxnorm = (1.0 - EPS_BALL) / jnp.sqrt(c)
            n = _norm(x)
            return jnp.where(n > maxnorm, x / n * maxnorm, x)

        def expmap0(u, c=C):
            sc = jnp.sqrt(c)
            n = _norm(u)
            return jnp.tanh(sc * n) * u / (sc * n)

        def logmap0(p, c=C):
            sc = jnp.sqrt(c)
            n = _norm(p)
            return jnp.arctanh(jnp.clip(sc * n, None, ARCTANH_CLIP)) * p / (sc * n)

        def mobius_add(x, y, c=C):
            x2 = jnp.sum(x * x, -1, keepdims=True)
            y2 = jnp.sum(y * y, -1, keepdims=True)
            xy = jnp.sum(x * y, -1, keepdims=True)
            num = (1.0 + 2.0 * c * xy + c * y2) * x + (1.0 - c * x2) * y
            den = 1.0 + 2.0 * c * xy + c * c * x2 * y2
            return num / jnp.clip(den, MIN_NORM, None)

        def mobius_matvec(W, x, c=C):
            sc = jnp.sqrt(c)
            xn = _norm(x)
            mx = x @ W.T
            mxn = _norm(mx)
            res = jnp.tanh(mxn / xn * jnp.arctanh(jnp.clip(sc * xn, None, ARCTANH_CLIP))) * mx / (mxn * sc)
            zero = jnp.all(mx == 0, axis=-1, keepdims=True)
            return jnp.where(zero, 0.0, res)

        def hyp_linear(x, W, b, c=C):
            mv = proj(mobius_matvec(W, x, c), c)
            bias = proj(expmap0(b[None, :], c), c)
            return proj(mobius_add(mv, bias, c), c)

        def hyp_agg(x, src, dst, w, n_nodes, c=C):
            xt = logmap0(x, c)
            msg = w[:, None] * xt[src]
            agg = jax.ops.segment_sum(msg, dst, num_segments=n_nodes)
            return proj(expmap0(agg, c), c)

        def hyp_act(x, c_in=C, c_out=C):
            xt = jax.nn.relu(logmap0(x, c_in))
            return proj(expmap0(xt, c_out), c_out)

        def hgcn_conv(x, src, dst, w, W, b, c_in=C, c_out=C):
            h = hyp_linear(x, W, b, c_in)
            h = hyp_agg(h, src, dst, w, x.shape[0], c_in)
            return hyp_act(h, c_in, c_out)
        src, dst = (edge_index[0], edge_index[1])
        h = proj(expmap0(x, C), C)
        h = hgcn_conv(h, src, dst, edge_weight, W1, b1, C, C)
        y = hgcn_conv(h, src, dst, edge_weight, W2, b2, C, C)
        return y

    def _L1_gnn_ref(features, edge_inputs, W, b, src, dst):
        import jax, jax.numpy as jnp
        import numpy as np
        N_NODES = 50000
        N_EDGES = 25000
        IN_DIM = 128
        P = 2
        OUT_DIM = 128
        n_nodes = features.shape[0]
        n_edges = edge_inputs.shape[0]
        p = edge_inputs.shape[1]
        in_dim = features.shape[1]
        h_src = features[src]
        msg_in = (edge_inputs[:, :, None] * h_src[:, None, :]).reshape(n_edges, p * in_dim)
        m = msg_in @ W.T + b
        h_out = jax.ops.segment_sum(m, dst, num_segments=n_nodes)
        return h_out
    edge_index = jnp.stack([src, dst])
    h = jnp.maximum(_layernorm(x, axis=-1), 0.0)
    x = x + _L0_gnn_ref(h, edge_index, edge_weight, L0_gnn_W1, L0_gnn_b1, L0_gnn_W2, L0_gnn_b2)
    h = jnp.maximum(_layernorm(x, axis=-1), 0.0)
    x = x + _L1_gnn_ref(h, edge_attr_2, L1_gnn_W, L1_gnn_b, src, dst)
    return x

_drawn_inputs = setup_inputs


def setup_inputs(seed=0):
    import zlib

    import numpy as np

    out = dict(_drawn_inputs(seed))
    spreads = {}
    factors = {'edge_weight': 2.728, 'L0_gnn_b1': 8.0}
    for name, (base, spread) in spreads.items():
        noise = np.random.default_rng([zlib.crc32(name.encode()), seed]).standard_normal(out[name].shape)
        drawn = base * np.exp(spread * noise) if base else spread * noise
        out[name] = jnp.asarray(drawn.astype(out[name].dtype))
    for name, factor in factors.items():
        out[name] = (out[name] * factor).astype(out[name].dtype)
    return out
```

```python
from contextlib import ExitStack, contextmanager

import numpy as np
import concourse.bass as bass
from concourse import mybir

F32 = mybir.dt.float32
BF16 = mybir.dt.bfloat16
I32 = mybir.dt.int32
U32 = mybir.dt.uint32
ALU = mybir.AluOpType
ACT = mybir.ActivationFunctionType
X = mybir.AxisListType.X

P = 128
D = 128
N = 50000
E = 50000
NT = -(-N // P)
ET = -(-E // P)
TAIL = N - (NT - 1) * P
NQ = -(-NT // 4)
ROWS = NQ * 4 * P
BLK = 4
COLS = BLK * P
PAD_DST = float(1 << 20)
RING = 10
AHEAD = 2
BEHIND = 8
PAIRS = 3
SLOTS = 4 * PAIRS + 1
GQ = 7
GT = 4 * GQ
NGRP = NQ // GQ
BALL = 1.0 - 0.004
ATANH_MAX = float(np.arctanh(BALL))
TINY = 1e-30
SMALL = 0.2

assert NQ == GQ * NGRP and NGRP % 2 == 0 and N == E


def at_least(eng, sem, value):
    if isinstance(value, int) and value <= 0:
        return
    eng.wait_ge(sem, value)


@contextmanager
def semaphores(nc, prefix):
    handed = []

    def sem(name):
        handed.append(nc.alloc_semaphore(name=f"{prefix}_{name}"))
        return handed[-1]

    yield sem
    nc.clear_and_free_semaphores(handed)
    nc.all_engine_barrier()


class Chain:

    def __init__(self, eng, sem, start):
        self.eng, self.sem, self.count = eng, sem, start

    def __call__(self, ins):
        ins.then_inc(self.sem, 1)
        self.count = self.count + 1
        self.eng.wait_ge(self.sem, self.count)


def over(ap, n):
    p, k = ap.shape
    return ap.unsqueeze(2).broadcast_to([p, k, n])


def under(ap, k):
    p, n = ap.shape
    return ap.unsqueeze(1).broadcast_to([p, k, n])


def tiles(ap):
    return ap.rearrange("p (t d) -> p t d", d=D)


RSQRT_MAGIC = float(0x5F3759DF)


def inverse_root(v, link, out, x, t):
    link(v.tensor_scalar(out.bitcast(I32), x.bitcast(I32), -0.5, RSQRT_MAGIC, ALU.mult, ALU.add))
    for _ in range(4):
        link(v.scalar_tensor_tensor(out=t, in0=out, scalar=-0.5, in1=out, op0=ALU.mult, op1=ALU.mult))
        link(v.tensor_tensor(t, t, x, ALU.mult))
        link(v.scalar_tensor_tensor(out=out, in0=t, scalar=1.5, in1=out, op0=ALU.add, op1=ALU.mult))


class Constants:

    def __init__(self, sb):
        self.ident = sb("ident", [P, P], F32)
        self.iota_row = sb("iota_row", [P, P], F32)
        self.earlier = sb("earlier", [P, P], F32)
        self.ones = sb("ones", [P, P], F32)
        self.zeros = sb("zeros", [P, 4 * D], F32)
        self.zero_row = sb("zero_row", [1, 4 * D], BF16)
        self.src_col = sb("src_col", [P, COLS], I32)
        self.dst_col = sb("dst_col", [P, COLS], F32)
        self.weight_col = sb("weight_col", [P, COLS], F32)
        self.attr_col = [sb(f"attr_col{i}", [P, COLS], F32) for i in range(2)]
        self.dst_in_tile = sb("dst_in_tile", [P, COLS, PAIRS], F32)
        self.slot_row = sb("slot_row", [1, COLS // 4, SLOTS], I32)
        self.slot_row_wide = sb("slot_row_wide", [1, COLS // 4, SLOTS], I32)
        self.slow = sb("slow", [1, 1], I32)
        self.trash = sb("trash", [P, 1], F32)
        self.w_t = [sb(f"w_t{i}", [P, D + 1], F32) for i in range(2)]
        self.bias = [sb(f"bias{i}", [P, D], F32) for i in range(2)]
        self.y2 = [sb(f"y2_{i}", [P, 1], F32) for i in range(2)]
        self.y2p1 = [sb(f"y2p1_{i}", [P, 1], F32) for i in range(2)]
        self.w_l1 = sb("w_l1", [P, 2 * D], F32)
        self.b_l1 = sb("b_l1", [P, D], F32)


def tables_pass(nc, c, io, dram):
    with semaphores(nc, "tb") as sem, ExitStack() as ctx:
        def sb(name, shape, dtype=F32):
            return ctx.enter_context(nc.sbuf_tensor("tb_" + name, shape, dtype))


        bank = [ctx.enter_context(nc.psum_tensor(f"tb_bank{i}", [P, 512], F32)) for i in range(8)]

        dst_int = sb("dst_int", [P, BLK, P], I32)
        next_int = sb("next_int", [P, BLK, P], I32)
        src_int = sb("src_int", [P, BLK, P], I32)
        weight = sb("weight", [P, BLK, P])
        attr = sb("attr", [P, BLK, 2 * P])
        attr_one = sb("attr_one", [P, 2, BLK, P])
        dst = sb("dst", [P, BLK, P])
        nxt = sb("nxt", [P, BLK, P])
        src = sb("src", [P, BLK, P])
        firsts = sb("firsts", [P, BLK, P])
        first_row = sb("first_row", [P, COLS])
        node0 = sb("node0", [P, 2, BLK])
        tile_no = sb("tile_no", [P, BLK])
        below = sb("below", [P, BLK, COLS])
        cnt = sb("cnt", [P, 2, BLK])
        need = sb("need", [P, PAIRS, BLK])
        need_idx = sb("need_idx", [P, PAIRS, BLK], I32)
        lap = sb("lap", [P, PAIRS, BLK])
        packed = sb("packed", [P, 2, BLK, 4])
        bad = sb("bad", [P, 3])
        next0, span, lead, live, wide, far, near = (
            sb(n, [P, BLK]) for n in ("next0", "span", "lead", "live", "wide", "far", "near"))
        needed = sb("needed", [P, PAIRS, BLK, P])
        slots = sb("slots", [1, 2, COLS * 4])
        any_third = sb("any_third", [1, COLS // 4])
        slow = sb("slow", [1, 1])
        w_nat = [sb(f"w_nat{i}", [P, D]) for i in range(2)]
        wl_nat = sb("wl_nat", [P, 2 * D])
        b_col = sb("b_col", [P, 2])
        squares = sb("squares", [P, 2, D])
        b_sum, b_clamp, b_inv, b_norm, b_tanh, b_scale = (
            sb(n, [P, 2]) for n in ("b_sum", "b_clamp", "b_inv", "b_norm", "b_tanh", "b_scale"))

        zeroed = sem("zeroed")
        loaded = sem("loaded")
        consts = sem("consts")
        dst_ready = sem("dst_ready")
        firsts_ready = sem("firsts_ready")
        first_ps = sem("first_ps")
        need_ready = sem("need_ready")
        rows_out = sem("rows_out")
        gathered = sem("gathered")
        slots_ready = sem("slots_ready")
        slots_out = sem("slots_out")
        slots_in = sem("slots_in")
        cols_ps = sem("cols_ps")
        cols_out = sem("cols_out")
        w_ps = sem("w_ps")
        rel_ready = sem("rel_ready")
        rel_ps = sem("rel_ps")
        b_norm_ready = sem("b_norm_ready")
        b_tanh_ready = sem("b_tanh_ready")
        b_col_ready = sem("b_col_ready")
        end_ps = sem("end_ps")
        dve_chain = sem("dve_chain")
        pool_chain = sem("pool_chain")

        whole = (BLK - 1) * P * P
        rest = (ET - 1) - (BLK - 1) * P
        rows_end = whole + rest * P

        with nc.Block() as block:
            @block.sync
            def _(sp):
                sp.wait_ge(zeroed, 5)
                lists = ((io["dst"], dst_int, 1, 0), (io["dst"], next_int, 1, 1), (io["src"], src_int, 1, 0),
                         (io["edge_weight"], weight, 1, 0), (io["edge_attr_2"].rearrange("e c -> (e c)"), attr, 2, 0))
                for vec, to, w, shift in lists:
                    a, b, end = shift + w * whole, shift + w * rows_end, w * E
                    sp.dma_start(to[:, 0:BLK - 1, :],
                                 vec[shift:a].rearrange("(b r l) -> r b l", r=P, l=w * P)).then_inc(loaded, 16)
                    sp.dma_start(to[0:rest, BLK - 1, :],
                                 vec[a:b].rearrange("(r l) -> r l", l=w * P)).then_inc(loaded, 16)
                    sp.dma_start(to[rest:rest + 1, BLK - 1, 0:end - b],
                                 vec[b:end].rearrange("(r l) -> r l", r=1)).then_inc(loaded, 16)
                for i, (w, bv) in enumerate(((io["W1"], io["b1"]), (io["W2"], io["b2"]))):
                    sp.dma_start(w_nat[i][:, :], w).then_inc(loaded, 16)
                    sp.dma_start(c.bias[i][:, :], bv.partition_broadcast(P)).then_inc(loaded, 16)
                    sp.dma_start(b_col[:, i:i + 1], bv.rearrange("(o u) -> o u", u=1)).then_inc(loaded, 16)
                sp.dma_start(wl_nat[:, :], io["W"]).then_inc(loaded, 16)
                sp.dma_start(c.b_l1[:, :], io["b"].partition_broadcast(P)).then_inc(loaded, 16)
                sp.wait_ge(dst_ready, 1)
                sp.dma_start(dram["dst_rows"].rearrange("(b r) l -> r b l", r=P), dst[:, :, :]).then_inc(rows_out, 16)
                sp.wait_ge(slots_ready, 1)
                for k in range(2):
                    sp.dma_start(dram["slots"][k].rearrange("(b r j) -> r b j", r=P, j=4),
                                 packed[:, k]).then_inc(slots_out, 16)
                sp.wait_ge(slots_out, 32)
                sp.dma_start(slots[0:1, :, :], dram["slots"].rearrange("(u k) n -> u k n", u=1)).then_inc(slots_in, 16)
                sp.wait_ge(slots_in, 16)

            loads = 15 + 8

            @block.gpsimd
            def _(pool):
                g = nc.gpsimd
                g.memset(dst_int[:, :, :], int(PAD_DST)).then_inc(zeroed, 1)
                g.memset(next_int[:, :, :], int(PAD_DST)).then_inc(zeroed, 1)
                g.memset(src_int[:, :, :], 0).then_inc(zeroed, 1)
                g.memset(weight[:, :, :], 0.0).then_inc(zeroed, 1)
                g.memset(attr[:, :, :], 0.0).then_inc(zeroed, 1)
                g.memset(c.zeros[:, :], 0.0)
                g.memset(c.zero_row[:, :], 0.0)
                g.memset(c.ones[:, :], 1.0).then_inc(pool_chain, 1)
                pool.wait_ge(pool_chain, 1)
                small = dict(allow_small_or_imprecise_dtypes=True)
                g.iota(c.iota_row[:, :], pattern=[[1, P]], base=0, channel_multiplier=0, **small)
                g.iota(c.trash[:, :], pattern=[[1, 1]], base=ROWS, channel_multiplier=1, **small)
                for j in range(2):
                    g.iota(node0[:, j, :], pattern=[[P * P, BLK]], base=P * j, channel_multiplier=P, **small)
                g.iota(tile_no[:, :], pattern=[[P, BLK]], base=0, channel_multiplier=1, **small)
                g.affine_select(out=c.ident[:, :], in_=c.ones[:, :], compare_op=ALU.is_equal, fill=0.0, base=0,
                                pattern=[[-1, P]], channel_multiplier=1)
                g.affine_select(out=c.earlier[:, :], in_=c.ones[:, :], compare_op=ALU.is_gt, fill=0.0, base=0,
                                pattern=[[-1, P]], channel_multiplier=1).then_inc(consts, 1)
                pool.wait_ge(need_ready, 1)
                pool.wait_ge(rows_out, 16)
                for j in range(PAIRS):
                    for b in range(BLK):
                        g.indirect_dma_start(out=needed[:, j, b, :], out_offset=None, in_=dram["dst_rows"],
                                             in_offset=bass.IndirectOffsetOnAxis(ap=need_idx[:, j, b:b + 1].bitcast(U32), axis=0)
                                             ).then_inc(gathered, 16)

            @block.tensor
            def _(pe):
                pe.wait_ge(consts, 1)
                pe.wait_ge(loaded, 16 * loads)
                pe.wait_ge(firsts_ready, 1)
                for b in range(BLK):
                    last = pe.matmul(bank[0][:, b * P:(b + 1) * P], c.ones[:, :], firsts[:, b, :], start=True, stop=True)
                last.then_inc(first_ps, 1)
                for n, have in enumerate((src, weight, attr_one[:, 0], attr_one[:, 1], dst)):
                    for b in range(BLK):
                        last = pe.transpose(bank[1 + n][:, b * P:(b + 1) * P], have[:, b, :], c.ident[:, :])
                last.then_inc(cols_ps, 1)
                for i in range(2):
                    pe.transpose(bank[6][:, i * P:(i + 1) * P], w_nat[i][:, :], c.ident[:, :])
                for i in range(2):
                    last = pe.transpose(bank[6][:, (2 + i) * P:(3 + i) * P], wl_nat[:, i * D:(i + 1) * D], c.ident[:, :])
                last.then_inc(w_ps, 1)
                pe.wait_ge(rel_ready, 1)
                pe.wait_ge(cols_out, 1)
                for j in range(PAIRS):
                    for b in range(BLK):
                        last = pe.transpose(bank[1 + j][:, b * P:(b + 1) * P], needed[:, j, b, :], c.ident[:, :])
                last.then_inc(rel_ps, 1)
                pe.wait_ge(b_col_ready, 1)
                for i in range(2):
                    pe.matmul(bank[7][:, i:i + 1], w_nat[i][:, :], b_col[:, i:i + 1], start=True, stop=True)
                pe.matmul(bank[7][0:1, 4:5], bad[:, 2:3], c.ones[:, 0:1], start=True, stop=True).then_inc(end_ps, 1)

            @block.scalar
            def _(act):
                act.wait_ge(b_norm_ready, 1)
                act.activation(b_tanh[:, :], b_norm[:, :], ACT.Tanh).then_inc(b_tanh_ready, 1)

            @block.vector
            def _(dve):
                v = nc.vector
                link = Chain(dve, dve_chain, 0)
                dve.wait_ge(consts, 1)
                dve.wait_ge(loaded, 16 * loads)
                v.tensor_copy(nxt[:, :, :], next_int[:, :, :])
                v.tensor_copy(src[:, :, :], src_int[:, :, :])
                for i in range(2):
                    v.tensor_copy(attr_one[:, i], attr[:, :, :].rearrange("p b (l a) -> p b l a", a=2)[:, :, :, i])
                link(v.tensor_copy(dst[:, :, :], dst_int[:, :, :]))
                dve.sem_inc(dst_ready, 1)
                link(v.tensor_tensor(firsts[:, :, :], under(c.ident[:, :], BLK), over(dst[:, :, 0], P), ALU.mult))
                dve.sem_inc(firsts_ready, 1)
                link(v.tensor_tensor(nxt[:, :, :], dst[:, :, :], nxt[:, :, :], ALU.is_gt))
                link(v.tensor_reduce(bad[:, 0:1], nxt[:, :, :].rearrange("p b l -> p (b l)"), X, ALU.add))
                dve.wait_ge(first_ps, 1)
                link(v.tensor_copy(first_row[:, :], bank[0][:, :]))
                for j in range(2):
                    link(v.tensor_tensor(below[:, :, :], under(first_row[:, :], BLK), over(node0[:, j, :], COLS), ALU.is_lt))
                    link(v.tensor_reduce(cnt[:, j, :], below[:, :, :], X, ALU.add))
                need0 = need[:, 0, :]
                v.tensor_scalar(need0, cnt[:, 0, :], -1.0, 0.0, ALU.add, ALU.max)
                link(v.tensor_scalar(next0[:, :], cnt[:, 1, :], -1.0, 0.0, ALU.add, ALU.max))
                for j in range(1, PAIRS):
                    v.tensor_scalar(need[:, j, :], need0, float(j), float(COLS - 1), ALU.add, ALU.min)
                v.tensor_tensor(span[:, :], next0[:, :], need0, ALU.subtract)
                link(v.tensor_tensor(lead[:, :], need0, tile_no[:, :], ALU.subtract))
                link(v.tensor_copy(need_idx[:, :, :], need[:, :, :]))
                dve.sem_inc(need_ready, 1)
                lap_of = float(4 * RING)
                link(v.tensor_scalar(lap[:, :, :], need[:, :, :], lap_of, None, ALU.is_ge))
                for k in range(2, COLS // (4 * RING) + 1):
                    link(v.scalar_tensor_tensor(out=lap[:, :, :], in0=need[:, :, :], scalar=lap_of * k,
                                                in1=lap[:, :, :], op0=ALU.is_ge, op1=ALU.add))
                link(v.scalar_tensor_tensor(out=lap[:, :, :], in0=lap[:, :, :], scalar=-lap_of,
                                            in1=need[:, :, :], op0=ALU.mult, op1=ALU.add))
                for k in range(2):
                    v.tensor_scalar(packed[:, k, :, 0:PAIRS], lap[:, :, :].rearrange("p j b -> p b j"),
                                    float(D * (k + 1)), None, ALU.mult)
                    last = v.tensor_scalar(packed[:, k, :, PAIRS], span[:, :], float(PAIRS - 1), None, ALU.is_ge)
                link(last)
                dve.sem_inc(slots_ready, 1)
                for i in range(2):
                    last = v.tensor_tensor(squares[:, i, :], c.bias[i][:, :], c.bias[i][:, :], ALU.mult)
                link(last)
                link(v.tensor_reduce(b_sum[:, :], squares[:, :, :], X, ALU.add))
                link(v.tensor_scalar(b_clamp[:, :], b_sum[:, :], TINY, None, ALU.max))
                inverse_root(v, link, b_inv[:, :], b_clamp[:, :], b_norm[:, :])
                v.tensor_scalar(live[:, :], tile_no[:, :], float(4 * NQ), None, ALU.is_lt)
                v.tensor_scalar(wide[:, :], span[:, :], float(PAIRS), None, ALU.is_ge)
                v.tensor_scalar(far[:, :], lead[:, :], float(4 * AHEAD - PAIRS + 1), None, ALU.is_gt)
                link(v.tensor_scalar(near[:, :], lead[:, :], float(-BEHIND), None, ALU.is_lt))
                link(v.tensor_tensor(wide[:, :], wide[:, :], far[:, :], ALU.add))
                link(v.tensor_tensor(wide[:, :], wide[:, :], near[:, :], ALU.add))
                link(v.tensor_tensor(wide[:, :], wide[:, :], live[:, :], ALU.mult))
                link(v.tensor_reduce(bad[:, 1:2], wide[:, :], X, ALU.add))
                link(v.tensor_tensor(bad[:, 2:3], bad[:, 0:1], bad[:, 1:2], ALU.add))
                dve.wait_ge(cols_ps, 1)
                for n, to in enumerate((c.src_col, c.weight_col, c.attr_col[0], c.attr_col[1], c.dst_col)):
                    last = v.tensor_copy(to[:, :], bank[1 + n][:, :])
                link(last)
                dve.sem_inc(cols_out, 1)
                dve.wait_ge(w_ps, 1)
                for i in range(2):
                    v.tensor_copy(c.w_t[i][:, 0:D], bank[6][:, i * P:(i + 1) * P])
                v.tensor_copy(c.w_l1[:, :], bank[6][:, 2 * P:4 * P])
                dve.wait_ge(gathered, 16 * PAIRS * BLK)
                for j in range(PAIRS):
                    last = v.tensor_tensor(needed[:, j], needed[:, j], over(node0[:, 0, :], P), ALU.subtract)
                link(last)
                dve.sem_inc(rel_ready, 1)
                link(v.tensor_tensor(b_norm[:, :], b_clamp[:, :], b_inv[:, :], ALU.mult))
                dve.sem_inc(b_norm_ready, 1)
                dve.wait_ge(b_tanh_ready, 1)
                link(v.tensor_scalar(b_tanh[:, :], b_tanh[:, :], BALL, None, ALU.min))
                link(v.tensor_tensor(b_scale[:, :], b_tanh[:, :], b_inv[:, :], ALU.mult))
                link(v.tensor_tensor(b_sum[:, :], b_sum[:, :], b_scale[:, :], ALU.mult))
                link(v.tensor_tensor(b_sum[:, :], b_sum[:, :], b_scale[:, :], ALU.mult))
                for i in range(2):
                    v.tensor_scalar(c.bias[i][:, :], c.bias[i][:, :], b_scale[:, i:i + 1], None, ALU.mult)
                    v.tensor_copy(c.y2[i][:, :], b_sum[:, i:i + 1])
                    v.tensor_scalar(c.y2p1[i][:, :], b_sum[:, i:i + 1], 1.0, None, ALU.add)
                link(v.tensor_tensor(b_col[:, :], b_col[:, :], b_scale[:, :], ALU.mult))
                dve.sem_inc(b_col_ready, 1)
                dve.wait_ge(rel_ps, 1)
                for j in range(PAIRS):
                    v.tensor_copy(c.dst_in_tile[:, :, j], bank[1 + j][:, :])
                dve.wait_ge(end_ps, 1)
                for i in range(2):
                    v.tensor_copy(c.w_t[i][:, D:D + 1], bank[7][:, i:i + 1])
                link(v.tensor_scalar(slow[:, :], bank[7][0:1, 4:5], 0.0, None, ALU.is_gt))
                link(v.tensor_copy(c.slow[:, :], slow[:, :]))
                dve.wait_ge(slots_in, 16)
                for k, row in enumerate((c.slot_row, c.slot_row_wide)):
                    by_quad = slots[:, k, :].rearrange("p (m r j) -> p m r j", r=4, j=4)
                    v.tensor_copy(row[:, :, 0:8].rearrange("p m (r j) -> p m r j", j=2), by_quad[:, :, :, 0:2])
                    v.tensor_copy(row[:, :, 9:13], by_quad[:, :, :, 2])
                    link(v.tensor_reduce(any_third[:, :], by_quad[:, :, :, PAIRS], X, ALU.max))
                    link(v.tensor_copy(row[:, :, 8], any_third[:, :]))


def hyper_pass(nc, c, name, layer, source, table, normed):
    with semaphores(nc, name) as sem, ExitStack() as ctx:
        def sb(n, shape, dtype=F32):
            return ctx.enter_context(nc.sbuf_tensor(f"{name}_{n}", shape, dtype))


        def banks(n, k):
            return [ctx.enter_context(nc.psum_tensor(f"{name}_{n}{i}", [P, 512], F32)) for i in range(k)]

        rows = [sb(f"rows{i}", [P, GT * D]) for i in range(2)]
        prod = [sb(f"prod{i}", [P, GT * D]) for i in range(2)]
        row_sq = sb("row_sq", [P, GT * D])
        prod_sq = sb("prod_sq", [P, GT * D])
        bias_part = sb("bias_part", [P, GT * D])
        turned = [sb(f"turned{i}", [P, 4 * P]) for i in range(2)]
        turn_ps = banks("turn_ps", 2)
        prod_ps = [ctx.enter_context(nc.psum_tensor(f"{name}_prod_ps{i}", [P, 2, 512], F32)) for i in range(2)]
        qb_raw = [sb(f"qb_raw{i}", [P, GT]) for i in range(2)]
        stats = sb("stats", [P, GT, 6])
        mean, var, gap = (sb(n, [P, GT]) for n in ("mean", "var", "gap"))
        roots, inv_roots, newton = (sb(n, [P, 3, GT]) for n in ("roots", "inv_roots", "newton"))
        dev = sb("dev", [P, GT])
        qsum = [sb(f"qsum{i}", [P, GT]) for i in range(2)]
        (inv_dev2, qb, clip, arg, th, mag, dirn, xy2, mag2, pn, den, al, be, n2, t1, t2, inv_n, nn, up, down,
         ratio, log, z, poly, small, f) = (sb(n, [P, GT]) for n in (
             "inv_dev2", "qb", "clip", "arg", "th", "mag", "dirn", "xy2", "mag2", "pn", "den", "al", "be", "n2",
             "t1", "t2", "inv_n", "nn", "up", "down", "ratio", "log", "z", "poly", "small", "f"))

        loaded = [sem(f"loaded{i}") for i in range(2)]
        tail_loaded = sem("tail_loaded")
        centred = sem("centred")
        turned_ps = sem("turned_ps")
        relued = sem("relued")
        multiplied = sem("multiplied")
        copied = sem("copied")
        lifted = sem("lifted")
        squared = sem("squared")
        summed = sem("summed")
        tanh_in, tanh_out = sem("tanh_in"), sem("tanh_out")
        log_in, log_out = sem("log_in"), sem("log_out")
        factors = sem("factors")
        scaled = sem("scaled")
        biased = sem("biased")
        finished = sem("finished")
        stored = [sem(f"stored{i}") for i in range(2)]
        dve_chain = sem("dve_chain")
        pool_chain = sem("pool_chain")

        has_tail = source.shape[0] < ROWS

        def quad(buf, k):
            return buf[:, 4 * D * k:4 * D * (k + 1)]

        def cols(buf, k):
            return buf[:, 4 * k:4 * (k + 1)]

        with nc.Block() as block:

            @block.sync
            def _(sp):
                def load(i, par):
                    if not (isinstance(i, int) and i < 2):
                        sp.wait_ge(turned_ps, GQ * (i - 1))
                        sp.wait_ge(squared, i - 1)
                    if has_tail and isinstance(i, int) and i == NGRP - 1:
                        first = GT * P * i
                        whole, some = divmod(N - first, GT)
                        sp.dma_start(rows[par][whole:whole + 1, 0:some * D], source[first + whole * GT:N, :].rearrange(
                            "(p t) d -> p (t d)", p=1)).then_inc(tail_loaded, 16)
                        sp.wait_ge(tail_loaded, 16)
                        sp.dma_start(rows[par][0:whole, :], source[first:first + whole * GT, :].rearrange(
                            "(p t) d -> p (t d)", t=GT)).then_inc(loaded[par], 16)
                    else:
                        sp.dma_start(rows[par][:, :], source[bass.ds(GT * P * i, GT * P), :].rearrange(
                            "(p t) d -> p (t d)", t=GT)).then_inc(loaded[par], 16)

                def store(i, par):
                    sp.wait_ge(finished, GQ * (i + 1))
                    sp.dma_start(table[bass.ds(GT * P * i, GT * P), :].rearrange("(p t) d -> p (t d)", t=GT),
                                 prod[par][:, :]).then_inc(stored[par], 16)

                load(0, 0)
                load(1, 1)
                def step(h, par):
                    load(2 * h + (2 + par), par)
                    store(2 * h + par, par)

                with sp.Fori(0, NGRP // 2 - 2) as h:
                    for par in range(2):
                        step(h, par)
                for par in range(2):
                    step(NGRP // 2 - 2, par)
                for par in range(2):
                    store(NGRP - 2 + par, par)
                for par in range(2):
                    sp.wait_ge(stored[par], 16 * (NGRP // 2))

            @block.gpsimd
            def _(pool):
                g = nc.gpsimd

                def squares(h, par):
                    i = 2 * h + par
                    if normed:
                        pool.wait_ge(lifted, GQ * (i + 1))
                        g.tensor_tensor(row_sq[:, :], row_sq[:, :], row_sq[:, :], ALU.mult).then_inc(squared, 1)
                    else:
                        pool.wait_ge(loaded[par], 16 * (h + 1))
                        at_least(pool, summed, i)
                        g.tensor_tensor(row_sq[:, :], rows[par][:, :], rows[par][:, :], ALU.mult).then_inc(squared, 1)

                def bias_parts(i, par):
                    pool.wait_ge(factors, i + 1)
                    at_least(pool, finished, GQ * i)
                    for k in range(GQ):
                        g.tensor_tensor(tiles(quad(bias_part, k)), under(c.bias[layer][:, :], 4), over(cols(be, k), D),
                                        ALU.mult).then_inc(biased, 1)
                    for k in range(GQ):
                        pool.wait_ge(scaled, GQ * i + k + 1)
                        pool.wait_ge(biased, GQ * i + k + 1)
                        g.tensor_tensor(quad(prod[par], k), quad(prod[par], k), quad(bias_part, k), ALU.add).then_inc(finished, 1)

                def step(h, par):
                    i = 2 * h + par
                    squares(h, par)
                    if not (isinstance(i, int) and i == 0):
                        bias_parts(i - 1, 1 - par)

                for par in range(2):
                    step(0, par)
                with pool.Fori(1, NGRP // 2) as h:
                    for par in range(2):
                        step(h, par)
                bias_parts(NGRP - 1, (NGRP - 1) % 2)

            @block.tensor
            def _(pe):
                def turn(h, par, k):
                    q = GQ * (2 * h + par) + k
                    if normed:
                        pe.wait_ge(centred, q + 1)
                    elif k == 0:
                        pe.wait_ge(loaded[par], 16 * (h + 1))
                    at_least(pe, relued, q - 1)
                    for r in range(4):
                        last = pe.transpose(turn_ps[(k + par) % 2][:, r * P:(r + 1) * P],
                                            rows[par][:, (4 * k + r) * D:(4 * k + r + 1) * D], c.ident[:, :])
                    last.then_inc(turned_ps, 1)

                def multiply(h, par, k):
                    i = 2 * h + par
                    q = GQ * i + k
                    slot = (k + par) % 2
                    pe.wait_ge(relued, q + 1)
                    at_least(pe, copied, q - 1)
                    for r in range(4):
                        r_t = turned[slot][:, r * P:(r + 1) * P]
                        last = pe.matmul(prod_ps[slot][:, r // 2, (r % 2) * (D + 1):(r % 2 + 1) * (D + 1)], r_t,
                                         c.w_t[layer][:, :], start=True, stop=True)
                    last.then_inc(multiplied, 1)

                def step(h, par):
                    for k in range(GQ):
                        turn(h, par, k)
                        if k:
                            multiply(h, par, k - 1)
                    multiply(h, par, GQ - 1)

                for par in range(2):
                    step(0, par)
                with pe.Fori(1, NGRP // 2) as h:
                    for par in range(2):
                        step(h, par)

            @block.scalar
            def _(act):
                def take_turned(h, par, k):
                    q = GQ * (2 * h + par) + k
                    slot = (k + par) % 2
                    act.wait_ge(turned_ps, q + 1)
                    at_least(act, multiplied, q - 1)
                    act.activation(turned[slot][:, :], turn_ps[slot][:, :], ACT.Relu).then_inc(relued, 1)

                def lift(h, par, k):
                    i = 2 * h + par
                    if k == 0:
                        at_least(act, summed, i)
                    act.wait_ge(centred, GQ * i + k + 1)
                    act.activation(quad(row_sq, k), quad(rows[par], k), ACT.Relu).then_inc(lifted, 1)

                def take_product(h, par, k):
                    i = 2 * h + par
                    q = GQ * i + k
                    slot = (k + par) % 2
                    act.wait_ge(multiplied, q + 1)
                    if k == 0:
                        at_least(act, stored[par], 16 * h)
                        at_least(act, summed, i)
                    both = prod_ps[slot][:, :, 0:2 * (D + 1)].rearrange("p a (b d) -> p a b d", b=2)
                    act.activation(quad(prod[par], k).rearrange("p (a b d) -> p a b d", a=2, b=2), both[:, :, :, 0:D], ACT.Copy)
                    act.activation(cols(qb_raw[par], k).rearrange("p (a b u) -> p a b u", a=2, u=1), both[:, :, :, D:D + 1], ACT.Copy)
                    for r in range(4):
                        t = 4 * k + r
                        last = act.activation(prod_sq[:, t * D:(t + 1) * D], both[:, r // 2, r % 2, 0:D],
                                              ACT.Square, accum_out=qsum[par][:, t:t + 1])
                    last.then_inc(copied, 1)

                def tanh(i):
                    act.wait_ge(tanh_in, i + 1)
                    act.activation(th[:, :], arg[:, :], ACT.Tanh).then_inc(tanh_out, 1)

                def logarithm(i):
                    act.wait_ge(log_in, i + 1)
                    act.activation(log[:, :], ratio[:, :], ACT.Ln).then_inc(log_out, 1)

                def step(h, par):
                    i = 2 * h + par
                    first = isinstance(i, int) and i == 0
                    if not first:
                        tanh(i - 1)
                    for k in range(GQ):
                        if normed:
                            lift(h, par, k)
                        take_turned(h, par, k)
                        if k:
                            take_product(h, par, k - 1)
                        if k == GQ - 2 and not first:
                            logarithm(i - 1)
                    take_product(h, par, GQ - 1)

                for par in range(2):
                    step(0, par)
                with act.Fori(1, NGRP // 2) as h:
                    for par in range(2):
                        step(h, par)
                tanh(NGRP - 1)
                logarithm(NGRP - 1)

            @block.vector
            def _(dve):
                v = nc.vector

                def centre(h, par, link):
                    i = 2 * h + par
                    x = tiles(rows[par][:, :])
                    dve.wait_ge(loaded[par], 16 * (h + 1))
                    for t in range(GT):
                        last = v.bn_stats(stats[:, t, :], x[:, t, :])
                    link(last)
                    link(v.tensor_tensor(mean[:, :], stats[:, :, 1], stats[:, :, 4], ALU.add))
                    link(v.tensor_scalar(mean[:, :], mean[:, :], 0.5, None, ALU.mult))
                    for k in range(GQ):
                        last = v.tensor_tensor(x[:, 4 * k:4 * k + 4, :], x[:, 4 * k:4 * k + 4, :],
                                               over(cols(mean, k), D), ALU.subtract)
                        last.then_inc(centred, 1)
                    v.tensor_tensor(gap[:, :], stats[:, :, 1], stats[:, :, 4], ALU.subtract)
                    link(v.tensor_tensor(var[:, :], stats[:, :, 2], stats[:, :, 5], ALU.add))
                    link(v.tensor_tensor(gap[:, :], gap[:, :], gap[:, :], ALU.mult))
                    link(v.tensor_scalar(var[:, :], var[:, :], 1.0 / D, 1e-5, ALU.mult, ALU.add))
                    link(v.scalar_tensor_tensor(out=dev[:, :], in0=gap[:, :], scalar=0.25, in1=var[:, :],
                                                op0=ALU.mult, op1=ALU.add))

                S, Q = roots[:, 0, :], roots[:, 1, :]
                inv_s, inv_q, inv_dev = inv_roots[:, 0, :], inv_roots[:, 1, :], inv_roots[:, 2, :]
                nroots = 3 if normed else 2

                def rapidity(i, par, link):
                    dve.wait_ge(squared, i + 1)
                    dve.wait_ge(copied, GQ * (i + 1))
                    v.tensor_copy(Q, qsum[par][:, :])
                    link(v.tensor_reduce(S, tiles(row_sq[:, :]), X, ALU.add))
                    dve.sem_inc(summed, 1)
                    if normed:
                        v.tensor_copy(roots[:, 2, :], dev[:, :])
                        link(v.reciprocal(inv_dev2[:, :], dev[:, :]))
                        link(v.tensor_tensor(roots[:, 0:2, :], roots[:, 0:2, :], under(inv_dev2[:, :], 2), ALU.mult))
                    link(v.tensor_scalar(roots[:, 0:nroots, :], roots[:, 0:nroots, :], TINY, None, ALU.max))
                    inverse_root(v, link, inv_roots[:, 0:nroots, :], roots[:, 0:nroots, :], newton[:, 0:nroots, :])
                    if normed:
                        v.tensor_tensor(qb[:, :], qb_raw[par][:, :], inv_dev, ALU.mult)
                    else:
                        v.tensor_copy(qb[:, :], qb_raw[par][:, :])
                    v.tensor_scalar(clip[:, :], inv_s, ATANH_MAX, 1.0, ALU.mult, ALU.min)
                    link(v.tensor_tensor(arg[:, :], Q, inv_q, ALU.mult))
                    link(v.tensor_tensor(arg[:, :], arg[:, :], clip[:, :], ALU.mult))
                    dve.sem_inc(tanh_in, 1)

                def factor(i, par, link):
                    dve.wait_ge(tanh_out, i + 1)
                    at_least(dve, biased, GQ * i)
                    link(v.tensor_scalar(mag[:, :], th[:, :], BALL, None, ALU.min))
                    v.tensor_tensor(mag2[:, :], mag[:, :], mag[:, :], ALU.mult)
                    link(v.tensor_tensor(dirn[:, :], mag[:, :], inv_q, ALU.mult))
                    link(v.scalar_tensor_tensor(out=xy2[:, :], in0=dirn[:, :], scalar=2.0, in1=qb[:, :], op0=ALU.mult, op1=ALU.mult))
                    v.tensor_scalar(pn[:, :], xy2[:, :], c.y2p1[layer][:, :], None, ALU.add)
                    v.scalar_tensor_tensor(out=den[:, :], in0=mag2[:, :], scalar=c.y2[layer][:, :], in1=xy2[:, :],
                                           op0=ALU.mult, op1=ALU.add)
                    link(v.tensor_scalar(be[:, :], mag2[:, :], -1.0, 1.0, ALU.mult, ALU.add))
                    v.tensor_tensor(al[:, :], pn[:, :], dirn[:, :], ALU.mult)
                    link(v.tensor_scalar(den[:, :], den[:, :], 1.0, 1e-15, ALU.add, ALU.max))
                    link(v.reciprocal(den[:, :], den[:, :]))
                    v.tensor_tensor(al[:, :], al[:, :], den[:, :], ALU.mult)
                    link(v.tensor_tensor(be[:, :], be[:, :], den[:, :], ALU.mult))
                    v.tensor_tensor(t1[:, :], al[:, :], al[:, :], ALU.mult)
                    v.tensor_tensor(t2[:, :], al[:, :], qb[:, :], ALU.mult)
                    link(v.tensor_scalar(n2[:, :], be[:, :], c.y2[layer][:, :], None, ALU.mult))
                    v.tensor_tensor(t1[:, :], t1[:, :], Q, ALU.mult)
                    link(v.scalar_tensor_tensor(out=t2[:, :], in0=t2[:, :], scalar=2.0, in1=n2[:, :], op0=ALU.mult, op1=ALU.add))
                    link(v.tensor_tensor(t2[:, :], t2[:, :], be[:, :], ALU.mult))
                    link(v.tensor_tensor(n2[:, :], t1[:, :], t2[:, :], ALU.add))
                    link(v.tensor_scalar(n2[:, :], n2[:, :], TINY, None, ALU.max))
                    inverse_root(v, link, inv_n[:, :], n2[:, :], t1[:, :])
                    link(v.tensor_tensor(nn[:, :], n2[:, :], inv_n[:, :], ALU.mult))
                    link(v.tensor_scalar(nn[:, :], nn[:, :], BALL, None, ALU.min))
                    v.tensor_scalar(up[:, :], nn[:, :], 1.0, None, ALU.add)
                    link(v.tensor_scalar(down[:, :], nn[:, :], -1.0, 1.0, ALU.mult, ALU.add))
                    link(v.reciprocal(down[:, :], down[:, :]))
                    link(v.tensor_tensor(ratio[:, :], up[:, :], down[:, :], ALU.mult))
                    dve.sem_inc(log_in, 1)
                    v.tensor_scalar(small[:, :], nn[:, :], SMALL, None, ALU.is_lt)
                    link(v.tensor_tensor(z[:, :], nn[:, :], nn[:, :], ALU.mult))
                    link(v.tensor_scalar(poly[:, :], z[:, :], 1.0 / 9, 1.0 / 7, ALU.mult, ALU.add))
                    link(v.tensor_tensor(poly[:, :], poly[:, :], z[:, :], ALU.mult))
                    link(v.scalar_tensor_tensor(out=poly[:, :], in0=poly[:, :], scalar=1.0 / 5, in1=z[:, :], op0=ALU.add, op1=ALU.mult))
                    link(v.scalar_tensor_tensor(out=poly[:, :], in0=poly[:, :], scalar=1.0 / 3, in1=z[:, :], op0=ALU.add, op1=ALU.mult))
                    link(v.scalar_tensor_tensor(out=poly[:, :], in0=poly[:, :], scalar=1.0, in1=nn[:, :], op0=ALU.add, op1=ALU.mult))
                    dve.wait_ge(log_out, i + 1)
                    link(v.scalar_tensor_tensor(out=poly[:, :], in0=log[:, :], scalar=-0.5, in1=poly[:, :], op0=ALU.mult, op1=ALU.add))
                    link(v.tensor_tensor(poly[:, :], poly[:, :], small[:, :], ALU.mult))
                    link(v.scalar_tensor_tensor(out=f[:, :], in0=log[:, :], scalar=0.5, in1=poly[:, :], op0=ALU.mult, op1=ALU.add))
                    link(v.tensor_tensor(f[:, :], f[:, :], inv_n[:, :], ALU.mult))
                    v.tensor_tensor(be[:, :], be[:, :], f[:, :], ALU.mult)
                    link(v.tensor_tensor(al[:, :], al[:, :], f[:, :], ALU.mult))
                    if normed:
                        link(v.tensor_tensor(al[:, :], al[:, :], inv_dev, ALU.mult))
                    dve.sem_inc(factors, 1)

                def scale(i, par, link):
                    for k in range(GQ):
                        q = tiles(quad(prod[par], k))
                        v.tensor_tensor(q, q, over(cols(al, k), D), ALU.mult).then_inc(scaled, 1)

                first_links = 7 if normed else 0
                step_links = [None]

                def step(h, par, links):
                    i = 2 * h + par
                    first = isinstance(i, int) and i == 0
                    link = Chain(dve, dve_chain, 0 if first else first_links + (i - 1) * links)
                    if not first:
                        rapidity(i - 1, 1 - par, link)
                    if normed:
                        centre(h, par, link)
                    if not first:
                        factor(i - 1, 1 - par, link)
                        scale(i - 1, 1 - par, link)
                    return link

                links = LINKS[normed]
                end = step(0, 0, links)
                assert end.count == first_links, end.count
                end = step(0, 1, links)
                assert end.count == first_links + links, end.count - first_links
                with dve.Fori(1, NGRP // 2) as h:
                    for par in range(2):
                        step(h, par, links)
                link = Chain(dve, dve_chain, first_links + (NGRP - 1) * links)
                rapidity(NGRP - 1, (NGRP - 1) % 2, link)
                factor(NGRP - 1, (NGRP - 1) % 2, link)
                scale(NGRP - 1, (NGRP - 1) % 2, link)


LINKS = {True: 68, False: 58}
RESIDUAL_LINKS = 35


def residual_pass(nc, c, name, sums, x, x2, table):
    with semaphores(nc, name) as sem, ExitStack() as ctx:
        def sb(n, shape, dtype=F32):
            return ctx.enter_context(nc.sbuf_tensor(f"{name}_{n}", shape, dtype))


        rows = [sb(f"rows{i}", [P, GT * D]) for i in range(2)]
        resid = [sb(f"resid{i}", [P, GT * D]) for i in range(2)]
        row_sq, relu_sq = sb("row_sq", [P, GT * D]), sb("relu_sq", [P, GT * D])
        turned = [sb(f"turned{i}", [P, 4 * P]) for i in range(2)]
        OUTS = GQ
        wide = [sb(f"wide{i}", [P, 4 * 2 * D]) for i in range(OUTS)]
        turn_ps = [ctx.enter_context(nc.psum_tensor(f"{name}_turn_ps{i}", [P, 512], F32)) for i in range(2)]
        prod_ps = [ctx.enter_context(nc.psum_tensor(f"{name}_prod_ps{i}", [P, 2, 512], F32)) for i in range(2)]
        stats = sb("stats", [P, GT, 6])
        roots, inv_roots, newton = (sb(n, [P, 2, GT]) for n in ("roots", "inv_roots", "newton"))
        mean, var, gap, clip, arg, th, gamma, dev, inv_dev, t1 = (sb(n, [P, GT]) for n in (
            "mean", "var", "gap", "clip", "arg", "th", "gamma", "dev", "inv_dev", "t1"))

        loaded = [sem(f"loaded{i}") for i in range(2)]
        tail_loaded = sem("tail_loaded")
        squared = sem("squared")
        relued = sem("relued")
        summed = sem("summed")
        tanh_in, tanh_out = sem("tanh_in"), sem("tanh_out")
        scaled = sem("scaled")
        added = sem("added")
        centred = sem("centred")
        normed = sem("normed")
        turned_ps = sem("turned_ps")
        taken = sem("taken")
        multiplied = sem("multiplied")
        copied = sem("copied")
        kept = [sem(f"kept{i}") for i in range(2)]
        stored = [sem(f"stored{i}") for i in range(OUTS)]
        dve_chain = sem("dve_chain")
        act_chain = sem("act_chain")

        def quad(buf, k):
            return buf[:, 4 * D * k:4 * D * (k + 1)]

        def cols(buf, k):
            return buf[:, 4 * k:4 * (k + 1)]

        def group(ap, i):
            return ap[bass.ds(GT * P * i, GT * P), :].rearrange("(p t) d -> p (t d)", t=GT)

        with nc.Block() as block:

            @block.sync
            def _(sp):
                def keep(i, par):
                    sp.wait_ge(added, GQ * (i + 1))
                    sp.dma_start(group(x2, i), resid[par][:, :]).then_inc(kept[par], 16)

                def store(i, par):
                    for k in range(GQ):
                        sp.wait_ge(copied, GQ * i + k + 1)
                        sp.dma_start(table[bass.ds(GT * P * i, GT * P), :].rearrange(
                            "(p t) d -> p t d", t=GT)[:, 4 * k:4 * k + 4, :].rearrange("p t d -> p (t d)"),
                            wide[k][:, :]).then_inc(stored[k], 16)

                def step(h, par, more):
                    i = 2 * h + par
                    keep(i, par)
                    store(i, par)
                    if more:
                        sp.wait_ge(kept[par], 16 * (h + 1))
                        sp.wait_ge(turned_ps, GQ * (i + 1))
                        load_into(2 * h + (2 + par), par)

                def load_into(i, par):
                    sp.dma_start(rows[par][:, :], group(sums, i)).then_inc(loaded[par], 16)
                    if isinstance(i, int) and i == NGRP - 1:
                        first = GT * P * i
                        whole, some = divmod(N - first, GT)
                        sp.dma_start(resid[par][whole:whole + 1, 0:some * D], x[first + whole * GT:N, :].rearrange(
                            "(p t) d -> p (t d)", p=1)).then_inc(tail_loaded, 16)
                        sp.wait_ge(tail_loaded, 16)
                        sp.dma_start(resid[par][0:whole, :], x[first:first + whole * GT, :].rearrange(
                            "(p t) d -> p (t d)", t=GT)).then_inc(loaded[par], 16)
                    else:
                        sp.dma_start(resid[par][:, :], group(x, i)).then_inc(loaded[par], 16)

                load_into(0, 0)
                load_into(1, 1)
                with sp.Fori(0, NGRP // 2 - 2) as h:
                    for par in range(2):
                        step(h, par, True)
                for par in range(2):
                    step(NGRP // 2 - 2, par, True)
                for par in range(2):
                    step(NGRP // 2 - 1, par, False)
                for par in range(2):
                    sp.wait_ge(kept[par], 16 * (NGRP // 2))
                for k in range(OUTS):
                    sp.wait_ge(stored[k], 16 * NGRP)

            @block.gpsimd
            def _(pool):
                g = nc.gpsimd

                def square(h, par):
                    i = 2 * h + par
                    pool.wait_ge(loaded[par], 32 * (h + 1))
                    at_least(pool, summed, i)
                    g.tensor_tensor(row_sq[:, :], rows[par][:, :], rows[par][:, :], ALU.mult).then_inc(squared, 1)

                def step(h, par, more):
                    i = 2 * h + par
                    for k in range(GQ):
                        pool.wait_ge(scaled, GQ * i + k + 1)
                        g.tensor_tensor(quad(resid[par], k), quad(resid[par], k), quad(rows[par], k), ALU.add).then_inc(added, 1)
                    if more:
                        square(h + par, 1 - par)
                    for k in range(GQ):
                        pool.wait_ge(centred, GQ * i + k + 1)
                        r = tiles(quad(rows[par], k))
                        g.tensor_tensor(r, r, over(cols(inv_dev, k), D), ALU.mult).then_inc(normed, 1)

                square(0, 0)
                for par in range(2):
                    step(0, par, True)
                with pool.Fori(1, NGRP // 2 - 1) as h:
                    for par in range(2):
                        step(h, par, True)
                for par in range(2):
                    step(NGRP // 2 - 1, par, par == 0)

            @block.tensor
            def _(pe):
                def turn(h, par, k):
                    q = GQ * (2 * h + par) + k
                    pe.wait_ge(normed, q + 1)
                    at_least(pe, taken, q - 1)
                    for r in range(4):
                        last = pe.transpose(turn_ps[(k + par) % 2][:, r * P:(r + 1) * P],
                                            rows[par][:, (4 * k + r) * D:(4 * k + r + 1) * D], c.ident[:, :])
                    last.then_inc(turned_ps, 1)

                def multiply(h, par, k):
                    q = GQ * (2 * h + par) + k
                    slot = (k + par) % 2
                    pe.wait_ge(taken, q + 1)
                    at_least(pe, copied, q - 1)
                    for r in range(4):
                        last = pe.matmul(prod_ps[slot][:, r // 2, (r % 2) * 2 * D:(r % 2 + 1) * 2 * D],
                                         turned[slot][:, r * P:(r + 1) * P], c.w_l1[:, :], start=True, stop=True)
                    last.then_inc(multiplied, 1)

                def step(h, par):
                    for k in range(GQ):
                        turn(h, par, k)
                        if k:
                            multiply(h, par, k - 1)
                    multiply(h, par, GQ - 1)

                for par in range(2):
                    step(0, par)
                with pe.Fori(1, NGRP // 2) as h:
                    for par in range(2):
                        step(h, par)

            @block.scalar
            def _(act):
                def relu(h, par):
                    i = 2 * h + par
                    act.wait_ge(squared, i + 1)
                    at_least(act, summed, i)
                    for k in range(GQ):
                        last = act.activation(quad(rows[par], k), quad(rows[par], k), ACT.Relu)
                    last.then_inc(act_chain, 1)
                    act.wait_ge(act_chain, i + 1)
                    for k in range(GQ):
                        last = act.activation(quad(relu_sq, k), quad(rows[par], k), ACT.Square)
                    last.then_inc(relued, 1)

                def tanh(i):
                    act.wait_ge(tanh_in, i + 1)
                    act.activation(th[:, :], arg[:, :], ACT.Tanh).then_inc(tanh_out, 1)

                def take(h, par, k):
                    q = GQ * (2 * h + par) + k
                    slot = (k + par) % 2
                    act.wait_ge(turned_ps, q + 1)
                    at_least(act, multiplied, q - 1)
                    act.activation(turned[slot][:, :], turn_ps[slot][:, :], ACT.Relu).then_inc(taken, 1)

                def copy(h, par, k):
                    i = 2 * h + par
                    act.wait_ge(multiplied, GQ * i + k + 1)
                    at_least(act, stored[k], 16 * i)
                    act.activation(wide[k][:, :].rearrange("p (a d) -> p a d", a=2), prod_ps[(k + par) % 2][:, :, :],
                                   ACT.Copy).then_inc(copied, 1)

                def step(h, par, more):
                    if more:
                        relu(h + par, 1 - par)
                    for k in range(GQ):
                        take(h, par, k)
                        if k:
                            copy(h, par, k - 1)
                        if k == 1 and more:
                            tanh(2 * h + par + 1)
                    copy(h, par, GQ - 1)

                relu(0, 0)
                tanh(0)
                for par in range(2):
                    step(0, par, True)
                with act.Fori(1, NGRP // 2 - 1) as h:
                    for par in range(2):
                        step(h, par, True)
                for par in range(2):
                    step(NGRP // 2 - 1, par, par == 0)

            @block.vector
            def _(dve):
                v = nc.vector
                S, R = roots[:, 0, :], roots[:, 1, :]
                inv_s, inv_r = inv_roots[:, 0, :], inv_roots[:, 1, :]

                def step(h, par):
                    i = 2 * h + par
                    link = Chain(dve, dve_chain, i * RESIDUAL_LINKS)
                    dve.wait_ge(squared, i + 1)
                    dve.wait_ge(relued, i + 1)
                    v.tensor_reduce(S, tiles(row_sq[:, :]), X, ALU.add)
                    link(v.tensor_reduce(R, tiles(relu_sq[:, :]), X, ALU.add))
                    dve.sem_inc(summed, 1)
                    link(v.tensor_scalar(roots[:, :, :], roots[:, :, :], TINY, None, ALU.max))
                    inverse_root(v, link, inv_roots[:, :, :], roots[:, :, :], newton[:, :, :])
                    v.tensor_scalar(clip[:, :], inv_s, ATANH_MAX, 1.0, ALU.mult, ALU.min)
                    link(v.tensor_tensor(arg[:, :], R, inv_r, ALU.mult))
                    link(v.tensor_tensor(arg[:, :], arg[:, :], clip[:, :], ALU.mult))
                    dve.sem_inc(tanh_in, 1)
                    dve.wait_ge(tanh_out, i + 1)
                    link(v.scalar_tensor_tensor(out=gamma[:, :], in0=th[:, :], scalar=BALL, in1=inv_r, op0=ALU.min, op1=ALU.mult))
                    for k in range(GQ):
                        r = tiles(quad(rows[par], k))
                        v.tensor_tensor(r, r, over(cols(gamma, k), D), ALU.mult).then_inc(scaled, 1)
                    res = tiles(resid[par][:, :])
                    for k in range(GQ):
                        dve.wait_ge(added, GQ * i + k + 1)
                        for t in range(4 * k, 4 * k + 4):
                            last = v.bn_stats(stats[:, t, :], res[:, t, :])
                    link(last)
                    v.tensor_tensor(gap[:, :], stats[:, :, 1], stats[:, :, 4], ALU.subtract)
                    v.tensor_tensor(var[:, :], stats[:, :, 2], stats[:, :, 5], ALU.add)
                    link(v.tensor_tensor(mean[:, :], stats[:, :, 1], stats[:, :, 4], ALU.add))
                    v.tensor_scalar(mean[:, :], mean[:, :], 0.5, None, ALU.mult)
                    v.tensor_scalar(var[:, :], var[:, :], 1.0 / D, 1e-5, ALU.mult, ALU.add)
                    link(v.tensor_tensor(gap[:, :], gap[:, :], gap[:, :], ALU.mult))
                    link(v.scalar_tensor_tensor(out=dev[:, :], in0=gap[:, :], scalar=0.25, in1=var[:, :],
                                                op0=ALU.mult, op1=ALU.add))
                    at_least(dve, normed, GQ * i)
                    inverse_root(v, link, inv_dev[:, :], dev[:, :], t1[:, :])
                    for k in range(GQ):
                        v.tensor_tensor(tiles(quad(rows[par], k)), res[:, 4 * k:4 * k + 4, :],
                                        over(cols(mean, k), D), ALU.subtract).then_inc(centred, 1)
                    return link.count

                count = step(0, 0)
                assert count == RESIDUAL_LINKS, count
                step(0, 1)
                with dve.Fori(1, NGRP // 2) as h:
                    for par in range(2):
                        step(h, par)


def edge_pass(nc, c, name, table, dst_rows, sums, out=None, x2=None):
    last = out is not None
    width = 2 * D if last else D
    with semaphores(nc, name) as sem, ExitStack() as ctx:
        def sb(n, shape, dtype=F32):
            return ctx.enter_context(nc.sbuf_tensor(f"{name}_{n}", shape, dtype))


        BANKS = RING // 2
        ring = sb("ring", [P, RING * 4 * width])
        index = sb("index", [P, RING * 4], I32)
        select = [sb(f"select{i}", [P, 4 * PAIRS, P]) for i in range(2)]
        stage = [sb(f"stage{i}", [P, 4 * D]) for i in range(BANKS)]
        sum_ps = [ctx.enter_context(nc.psum_tensor(f"{name}_sum_ps{i}", [P, 512], F32)) for i in range(BANKS)]

        landed = [sem(f"landed{i}") for i in range(RING)]
        may_gather = sem("may_gather")
        indexed = sem("indexed")
        weighed = sem("weighed")
        messages = sem("messages")
        selected = sem("selected")
        added = sem("added")
        taken = sem("taken")
        x2_in = [sem(f"x2_in{i}") for i in range(BANKS)] if last else None
        stored = [sem(f"stored{i}") for i in range(BANKS)]
        dve_chain = sem("dve_chain")

        groups = -(-NQ // RING)
        spare = 9

        def over_groups(eng, step):
            def body(g):
                for k in range(RING):
                    if not (isinstance(g, int) and RING * g + k >= NQ):
                        step(g, k)
            body(0)
            with eng.Fori(1, groups - 1) as g:
                body(g)
            body(groups - 1)

        def exists(q):
            return not (isinstance(q, int) and q >= NQ)

        def wait_landed(eng, g, k):
            g, k = (g, k) if k < RING else (g + 1, k - RING)
            short = isinstance(g, int) and RING * g + k == NQ - 1
            eng.wait_ge(landed[k], 64 * (g + 1) - (16 * (4 * NQ - ET) if short else 0))

        def ring_quad(k):
            return ring[:, (k % RING) * 4 * width:(k % RING + 1) * 4 * width].rearrange("p (t d) -> p t d", d=width)

        def node_rows(ap, q):
            return ap[bass.ds(4 * P * q, 4 * P), :].rearrange("(t p) d -> p t d", p=P)


        def fast_pool(pool):
            def step(g, k):
                q = RING * g + k
                pool.wait_ge(indexed, q + 1)
                if not (isinstance(g, int) and g == 0):
                    pool.wait_ge(added, q - RING + AHEAD + 1)
                pool.sem_inc(may_gather, 1)
                for t in range(4):
                    if isinstance(g, int) and 4 * q + t >= ET:
                        break
                    at = 4 * k + t
                    nc.gpsimd.indirect_dma_start(
                        out=ring[:, at * width:(at + 1) * width], out_offset=None, in_=table,
                        in_offset=bass.IndirectOffsetOnAxis(ap=index[:, at:at + 1].bitcast(U32), axis=0)).then_inc(landed[k], 16)

            over_groups(pool, step)

        def fast_pe(pe):
            slots = c.slot_row_wide if last else c.slot_row

            def load(numbers):
                return nc.values_load_multi_w_load_instructions(
                    numbers, engines=(mybir.EngineType.PE,), min_val=0, max_val=(4 * RING - 1) * width)[1]

            def step(g, k):
                q = RING * g + k
                numbers = load(slots[0:1, bass.ds(q, 1), 0:9])
                use_third = numbers[8]
                if isinstance(q, int):
                    pe.wait_ge(messages, min(q + AHEAD + 1, NQ))
                else:
                    pe.wait_ge(messages, q + AHEAD + 1)
                pe.wait_ge(selected, q + 1)
                at_least(pe, taken, q - BANKS + 1)

                def pair(r, j, where, **flags):
                    return pe.matmul(sum_ps[k % BANKS][:, r * D:(r + 1) * D], select[k % 2][:, PAIRS * r + j, :],
                                     ring[:, bass.ds(where, D)], **flags)

                pe.matmul(sum_ps[k % BANKS][:, :], c.zero_row[0:1, 0:P], c.zero_row[0:1, :], start=True, stop=False)
                with pe.If(use_third > 0):
                    third = load(slots[0:1, bass.ds(q, 1), 9:13])
                    for r in range(4):
                        pair(r, 2, third[r], start=False, stop=False)
                for r in range(4):
                    for j in range(2):
                        mm = pair(r, j, numbers[2 * r + j], start=False, stop=r == 3 and j == 1)
                mm.then_inc(added, 1)

            over_groups(pe, step)

        def fast_act(act):
            def fill_index(q, k):
                src = c.src_col[:, bass.ds(4 * q, 4)]
                act.activation(index[:, 4 * (k % RING):4 * (k % RING) + 4], src, ACT.Copy).then_inc(indexed, 1)

            def weigh(g, k):
                q = RING * g + k
                wait_landed(act, g, k)
                for t in range(4):
                    half = ring_quad(k)[:, t, D:2 * D]
                    ins = act.activation(half, half, ACT.Copy, scale=c.attr_col[1][:, bass.ds(4 * q + t, 1)])
                ins.then_inc(weighed, 1)

            def step(g, k):
                q = RING * g + k
                if last:
                    if exists(q + AHEAD):
                        weigh(g, k + AHEAD)
                else:
                    act.wait_ge(added, q + 1)
                    at_least(act, stored[k % BANKS], 16 * (2 * g + k // BANKS))
                    act.activation(stage[k % BANKS][:, :], sum_ps[k % BANKS][:, :], ACT.Copy).then_inc(taken, 1)
                if exists(q + spare):
                    fill_index(q + spare, k + spare)

            for q in range(spare):
                fill_index(q, q)
            if last:
                for q in range(AHEAD):
                    weigh(0, q)
            over_groups(act, step)

        def fast_dve(dve):
            v = nc.vector

            def message(g, k, q):
                wait_landed(dve, g, k)
                m = ring_quad(k)[:, :, 0:D]
                if last:
                    v.tensor_tensor(m, m, over(c.attr_col[0][:, bass.ds(4 * q, 4)], D), ALU.mult).then_inc(dve_chain, 1)
                else:
                    v.tensor_tensor(m, m, over(c.weight_col[:, bass.ds(4 * q, 4)], D), ALU.mult).then_inc(messages, 1)

            def message_rest(k, q):
                m = ring_quad(k)[:, :, 0:D]
                dve.wait_ge(weighed, q + 1)
                dve.wait_ge(dve_chain, 2 * q + 1)
                v.tensor_tensor(m, m, ring_quad(k)[:, :, D:2 * D], ALU.add).then_inc(dve_chain, 1)
                dve.wait_ge(dve_chain, 2 * q + 2)
                v.tensor_tensor(m, m, under(c.b_l1[:, :], 4), ALU.add).then_inc(messages, 1)

            def finish(g, k, q):
                dve.wait_ge(added, q + 1)
                dve.wait_ge(x2_in[k % BANKS], 32 * (2 * g + k // BANKS + 1))
                v.tensor_tensor(stage[k % BANKS][:, :], stage[k % BANKS][:, :], sum_ps[k % BANKS][:, :], ALU.add).then_inc(taken, 1)

            def step(g, k):
                q = RING * g + k
                if exists(q + AHEAD):
                    message(g, k + AHEAD, q + AHEAD)
                at_least(dve, added, q - 1)
                rel = c.dst_in_tile[:, bass.ds(4 * q, 4), :].rearrange("p t j -> p (t j)")
                v.tensor_tensor(select[k % 2][:, :, :], under(c.iota_row[:, :], 4 * PAIRS), over(rel, P),
                                ALU.is_equal).then_inc(selected, 1)
                if last:
                    if exists(q + AHEAD):
                        message_rest(k + AHEAD, q + AHEAD)
                    if not (isinstance(q, int) and q == 0):
                        finish(*((g, k - 1) if k else (g - 1, RING - 1)), q - 1)

            for q in range(AHEAD):
                message(0, q, q)
                if last:
                    message_rest(q, q)
            over_groups(dve, step)
            if last:
                finish(groups - 1, (NQ - 1) % RING, NQ - 1)

        def fast_sp(sp):
            def load_x2(g, k, q):
                slot = k % BANKS
                if not (isinstance(q, int) and q < BANKS):
                    sp.wait_ge(stored[slot], 16 * (2 * g + (k // BANKS)))
                for half in range(2):
                    part = slice(64 * half, 64 * half + 64)
                    sp.dma_start(tiles(stage[slot][:, :])[part], node_rows(x2, q)[part]).then_inc(x2_in[slot], 16)

            def step(g, k):
                q = RING * g + k
                slot = k % BANKS
                if last:
                    if exists(q + 3):
                        load_x2(*((g, k + 3) if k + 3 < RING else (g + 1, k + 3 - RING)), q + 3)
                sp.wait_ge(taken, q + 1)
                if last and isinstance(q, int) and q == NQ - 1:
                    whole = NT - 1 - 4 * q
                    first = 4 * P * q
                    sp.dma_start(out[first:first + whole * P, :].rearrange("(t p) d -> p t d", p=P),
                                 tiles(stage[slot][:, :])[:, 0:whole, :]).then_inc(stored[slot], 16)
                    sp.dma_start(out[first + whole * P:N, :],
                                 stage[slot][0:TAIL, whole * D:(whole + 1) * D]).then_inc(stored[slot], 16)
                else:
                    sp.dma_start(node_rows(out if last else sums, q), tiles(stage[slot][:, :])).then_inc(stored[slot], 16)

            if last:
                for q in range(3):
                    load_x2(0, q, q)
            over_groups(sp, step)
            for slot in range(BANKS):
                uses = len(range(slot, NQ, BANKS)) + (1 if last and (NQ - 1) % BANKS == slot else 0)
                sp.wait_ge(stored[slot], 16 * uses)

        s_index, s_target = sb("s_index", [P, 1], I32), sb("s_target", [P, 1], I32)
        s_rows, s_message = sb("s_rows", [P, D]), sb("s_message", [P, width])
        s_dst, s_same, s_before = sb("s_dst", [P, P]), sb("s_same", [P, P]), sb("s_before", [P, P])
        s_first, s_real, s_goal = sb("s_first", [P, 1]), sb("s_real", [P, 1]), sb("s_goal", [P, 1])
        s_zeroed = sem("s_zeroed")
        s_indexed = sem("s_indexed")
        s_gathered = sem("s_gathered")
        s_dst_in = sem("s_dst_in")
        s_targeted = sem("s_targeted")
        s_ready = sem("s_ready")
        s_summed = sem("s_summed")
        s_fetched = sem("s_fetched")
        s_added = sem("s_added")
        s_written = sem("s_written")
        s_chain = sem("s_chain")
        OUT_P, OUT_T = 125, 4
        chunks = N // (OUT_P * OUT_T)

        def over_tiles(eng, step, n):
            step(0)
            with eng.Fori(1, n) as e:
                step(e)

        def slow_sp(sp):
            def zero(q):
                sp.dma_start(sums[bass.ds(4 * P * q, 4 * P), :].rearrange("(p t) d -> p (t d)", t=4), c.zeros[:, :]).then_inc(s_zeroed, 16)

            with sp.Fori(0, NQ) as q:
                zero(q)
            sp.dma_start(sums[ROWS:ROWS + P, :], c.zeros[:, 0:D]).then_inc(s_zeroed, 16)

            def step(e):
                at_least(sp, s_written, 16 * e)
                sp.dma_start(s_dst[:, :], dst_rows[bass.ds(e, 1), :].broadcast_to([P, P])).then_inc(s_dst_in, 16)

            over_tiles(sp, step, ET)
            sp.wait_ge(s_written, 16 * ET)
            if last:
                def chunk(ap, n):
                    return ap[bass.ds(OUT_P * OUT_T * n, OUT_P * OUT_T), :].rearrange("(p t) d -> p (t d)", t=OUT_T)

                def finish(n):
                    at_least(sp, stored[0], 16 * n)
                    sp.dma_start(stage[0][0:OUT_P, :], chunk(sums, n)).then_inc(x2_in[0], 16)
                    sp.dma_start(stage[1][0:OUT_P, :], chunk(x2, n)).then_inc(x2_in[0], 16)
                    sp.wait_ge(taken, n + 1)
                    sp.dma_start(chunk(out, n), stage[0][0:OUT_P, :]).then_inc(stored[0], 16)

                over_tiles(sp, finish, chunks)
                sp.wait_ge(stored[0], 16 * chunks)

        def slow_pool(pool):
            def step(e):
                pool.wait_ge(s_indexed, e + 1)
                pool.sem_inc(may_gather, 1)
                nc.gpsimd.indirect_dma_start(out=s_message[:, :], out_offset=None, in_=table, in_offset=bass.IndirectOffsetOnAxis(
                    ap=s_index[:, 0:1].bitcast(U32), axis=0)).then_inc(s_gathered, 16)
                pool.wait_ge(s_targeted, e + 1)
                if isinstance(e, int) and e == 0:
                    pool.wait_ge(s_zeroed, 16 * (NQ + 1))
                pool.sem_inc(may_gather, 1)
                nc.gpsimd.indirect_dma_start(out=s_rows[:, :], out_offset=None, in_=sums, in_offset=bass.IndirectOffsetOnAxis(
                    ap=s_target[:, 0:1].bitcast(U32), axis=0)).then_inc(s_fetched, 16)
                pool.wait_ge(s_added, e + 1)
                pool.sem_inc(may_gather, 1)
                nc.gpsimd.indirect_dma_start(out=sums, out_offset=bass.IndirectOffsetOnAxis(
                    ap=s_target[:, 0:1].bitcast(U32), axis=0), in_=s_rows[:, :], in_offset=None).then_inc(s_written, 16)
                pool.wait_ge(s_written, 16 * (e + 1))

            over_tiles(pool, step, ET)

        def slow_pe(pe):
            def step(e):
                pe.wait_ge(s_ready, e + 1)
                pe.matmul(sum_ps[0][:, 0:D], s_same[:, :], s_message[:, 0:D], start=True, stop=True).then_inc(s_summed, 1)

            over_tiles(pe, step, ET)

        def slow_dve(dve):
            v = nc.vector
            links = 5 + (3 if last else 1)

            def step(e):
                link = Chain(dve, s_chain, links * e)
                dst = c.dst_col[:, bass.ds(e, 1)]
                at_least(dve, s_written, 16 * e)
                v.tensor_copy(s_index[:, :], c.src_col[:, bass.ds(e, 1)]).then_inc(s_indexed, 1)
                dve.wait_ge(s_dst_in, 16 * (e + 1))
                v.tensor_scalar(s_real[:, :], dst, float(N), None, ALU.is_lt)
                v.tensor_tensor(s_goal[:, :], dst, c.trash[:, :], ALU.subtract)
                link(v.tensor_scalar(s_same[:, :], s_dst[:, :], dst, None, ALU.is_equal))
                link(v.tensor_tensor(s_before[:, :], s_same[:, :], c.earlier[:, :], ALU.mult))
                link(v.tensor_reduce(s_first[:, :], s_before[:, :], X, ALU.add))
                link(v.scalar_tensor_tensor(out=s_first[:, :], in0=s_first[:, :], scalar=0.0, in1=s_real[:, :],
                                            op0=ALU.is_equal, op1=ALU.mult))
                link(v.scalar_tensor_tensor(out=s_goal[:, :], in0=s_goal[:, :], scalar=s_first[:, 0:1], in1=c.trash[:, :],
                                            op0=ALU.mult, op1=ALU.add))
                v.tensor_copy(s_target[:, :], s_goal[:, :]).then_inc(s_targeted, 1)
                dve.wait_ge(s_gathered, 16 * (e + 1))
                m = s_message[:, 0:D]
                if last:
                    link(v.tensor_scalar(m, m, c.attr_col[0][:, bass.ds(e, 1)], None, ALU.mult))
                    link(v.scalar_tensor_tensor(out=m, in0=s_message[:, D:2 * D], scalar=c.attr_col[1][:, bass.ds(e, 1)], in1=m,
                                                op0=ALU.mult, op1=ALU.add))
                    link(v.tensor_tensor(m, m, c.b_l1[:, :], ALU.add))
                else:
                    link(v.tensor_scalar(m, m, c.weight_col[:, bass.ds(e, 1)], None, ALU.mult))
                dve.sem_inc(s_ready, 1)
                dve.wait_ge(s_summed, e + 1)
                dve.wait_ge(s_fetched, 16 * (e + 1))
                v.tensor_tensor(s_rows[:, :], s_rows[:, :], sum_ps[0][:, 0:D], ALU.add).then_inc(s_added, 1)

            over_tiles(dve, step, ET)
            if last:
                def finish(n):
                    dve.wait_ge(x2_in[0], 32 * (n + 1))
                    v.tensor_tensor(stage[0][0:OUT_P, :], stage[0][0:OUT_P, :], stage[1][0:OUT_P, :], ALU.add).then_inc(taken, 1)

                over_tiles(dve, finish, chunks)

        def either(eng, slow, fast):
            is_slow = eng.value_load(c.slow[0:1, 0:1], min_val=0, max_val=1)
            with eng.If(is_slow > 0):
                slow(eng)
            with eng.Else():
                fast(eng)

        with nc.Block() as block:

            @block.sync
            def _(sp):
                either(sp, slow_sp, fast_sp)

            @block.gpsimd
            def _(pool):
                either(pool, slow_pool, fast_pool)

            @block.tensor
            def _(pe):
                either(pe, slow_pe, fast_pe)

            @block.vector
            def _(dve):
                either(dve, slow_dve, fast_dve)

            @block.scalar
            def _(act):
                is_slow = act.value_load(c.slow[0:1, 0:1], min_val=0, max_val=1)
                with act.If(is_slow < 1):
                    fast_act(act)


def build(nc, x, src, dst, edge_attr_2, edge_weight, W1, b1, W2, b2, W, b, out):
    with ExitStack() as ctx:
        def scratch(name, shape):
            return nc.dram_tensor(name, shape, F32, kind="Internal").ap()

        c = Constants(lambda n, s, d: ctx.enter_context(nc.sbuf_tensor(n, s, d)))
        io = dict(x=x, src=src, dst=dst, edge_attr_2=edge_attr_2, edge_weight=edge_weight, W1=W1, b1=b1, W2=W2, b2=b2, W=W, b=b)
        dram = dict(dst_rows=scratch("dst_rows", (COLS, P)), slots=scratch("slots", (2, COLS * 4)))
        table = scratch("table", (ROWS, D))
        sums = scratch("sums", (ROWS + P, D))
        x2 = scratch("x2", (ROWS, D))
        wide = scratch("wide", (ROWS, 2 * D))
        tables_pass(nc, c, io, dram)
        hyper_pass(nc, c, "la", 0, x, table, True)
        edge_pass(nc, c, "ea", table, dram["dst_rows"], sums)
        hyper_pass(nc, c, "lb", 1, sums, table, False)
        edge_pass(nc, c, "eb", table, dram["dst_rows"], sums)
        residual_pass(nc, c, "rs", sums, x, x2, wide)
        edge_pass(nc, c, "ec", wide, dram["dst_rows"], sums, out, x2)


_INS = ["x", "src", "dst", "edge_attr_2", "edge_weight", "L0_gnn_W1", "L0_gnn_b1", "L0_gnn_W2", "L0_gnn_b2", "L1_gnn_W", "L1_gnn_b"]


def kernel(**inputs):
    import numpy as _np
    import concourse.bacc as _bacc
    from concourse import mybir as _mybir
    from concourse.bass_utils import run_bass_kernel_spmd as _run

    nc = _bacc.Bacc("TRN2", target_bir_lowering=False, num_devices=1)
    arrays, args = {}, []
    for name in _INS:
        a = _np.ascontiguousarray(inputs[name])
        arrays[f"in_{name}"] = a
        args.append(nc.dram_tensor(f"in_{name}", a.shape, _mybir.dt.from_np(a.dtype), kind="ExternalInput").ap())
    args.append(nc.dram_tensor("out_0", (N, D), F32, kind="ExternalOutput").ap())
    build(nc, *args)
    return _run(nc, [arrays], core_ids=[0]).results[0]["out_0"]
```

```python
from contextlib import ExitStack, contextmanager

import numpy as np
import concourse.bass as bass
from concourse import mybir

F32 = mybir.dt.float32
BF16 = mybir.dt.bfloat16
I32 = mybir.dt.int32
U32 = mybir.dt.uint32
ALU = mybir.AluOpType
ACT = mybir.ActivationFunctionType
X = mybir.AxisListType.X

P = 128
D = 128
N = 50000
E = 50000
NT = -(-N // P)
ET = -(-E // P)
TAIL = N - (NT - 1) * P
NQ = -(-NT // 4)
ROWS = NQ * 4 * P
BLK = 4
COLS = BLK * P
PAD_DST = float(1 << 20)
RING = 10
AHEAD = 2
BEHIND = 8
PAIRS = 3
SLOTS = 4 * PAIRS + 1
GQ = 7
GT = 4 * GQ
NGRP = NQ // GQ
BALL = 1.0 - 0.004
ATANH_MAX = float(np.arctanh(BALL))
TINY = 1e-30
SMALL = 0.2

assert NQ == GQ * NGRP and NGRP % 2 == 0 and N == E


def at_least(eng, sem, value):
    if isinstance(value, int) and value <= 0:
        return
    eng.wait_ge(sem, value)


@contextmanager
def semaphores(nc, prefix):
    handed = []

    def sem(name):
        handed.append(nc.alloc_semaphore(name=f"{prefix}_{name}"))
        return handed[-1]

    yield sem
    nc.clear_and_free_semaphores(handed)
    nc.all_engine_barrier()


class Chain:

    def __init__(self, eng, sem, start):
        self.eng, self.sem, self.count = eng, sem, start
        self.meanwhile, self.n = None, 0

    def beside(self, meanwhile):
        self.meanwhile, self.n = meanwhile, 0

    def __call__(self, ins):
        ins.then_inc(self.sem, 1)
        if self.meanwhile is not None:
            self.meanwhile(self.n)
            self.n += 1
        self.count = self.count + 1
        self.eng.wait_ge(self.sem, self.count)


def over(ap, n):
    p, k = ap.shape
    return ap.unsqueeze(2).broadcast_to([p, k, n])


def under(ap, k):
    p, n = ap.shape
    return ap.unsqueeze(1).broadcast_to([p, k, n])


def tiles(ap):
    return ap.rearrange("p (t d) -> p t d", d=D)


RSQRT_MAGIC = float(0x5F3759DF)


def inverse_root(v, link, out, x, t):
    link(v.tensor_scalar(out.bitcast(I32), x.bitcast(I32), -0.5, RSQRT_MAGIC, ALU.mult, ALU.add))
    for _ in range(3):
        link(v.scalar_tensor_tensor(out=t, in0=out, scalar=-0.5, in1=out, op0=ALU.mult, op1=ALU.mult))
        link(v.tensor_tensor(t, t, x, ALU.mult))
        link(v.scalar_tensor_tensor(out=out, in0=t, scalar=1.5, in1=out, op0=ALU.add, op1=ALU.mult))


class Constants:

    def __init__(self, sb):
        self.ident = sb("ident", [P, P], F32)
        self.iota_row = sb("iota_row", [P, P], F32)
        self.earlier = sb("earlier", [P, P], F32)
        self.ones = sb("ones", [P, P], F32)
        self.zeros = sb("zeros", [P, 4 * D], F32)
        self.zero_row = sb("zero_row", [1, 4 * D], BF16)
        self.src_col = sb("src_col", [P, COLS], I32)
        self.dst_col = sb("dst_col", [P, COLS], F32)
        self.weight_col = sb("weight_col", [P, COLS], F32)
        self.attr_col = [sb(f"attr_col{i}", [P, COLS], F32) for i in range(2)]
        self.dst_in_tile = sb("dst_in_tile", [P, COLS, PAIRS], F32)
        self.slot_row = sb("slot_row", [1, COLS // 4, SLOTS], I32)
        self.slot_row_wide = sb("slot_row_wide", [1, COLS // 4, SLOTS], I32)
        self.slow = sb("slow", [1, 1], I32)
        self.trash = sb("trash", [P, 1], F32)
        self.w_t = [sb(f"w_t{i}", [P, D + 1], F32) for i in range(2)]
        self.bias = [sb(f"bias{i}", [P, D], F32) for i in range(2)]
        self.y2 = [sb(f"y2_{i}", [P, 1], F32) for i in range(2)]
        self.y2p1 = [sb(f"y2p1_{i}", [P, 1], F32) for i in range(2)]
        self.w_l1 = sb("w_l1", [P, 2 * D], F32)
        self.b_l1 = sb("b_l1", [P, D], F32)


def tables_pass(nc, c, io, dram):
    with semaphores(nc, "tb") as sem, ExitStack() as ctx:
        def sb(name, shape, dtype=F32):
            return ctx.enter_context(nc.sbuf_tensor("tb_" + name, shape, dtype))

        bank = [ctx.enter_context(nc.psum_tensor(f"tb_bank{i}", [P, 512], F32)) for i in range(8)]

        dst_int = sb("dst_int", [P, BLK, P], I32)
        next_int = sb("next_int", [P, BLK, P], I32)
        src_int = sb("src_int", [P, BLK, P], I32)
        weight = sb("weight", [P, BLK, P])
        attr = sb("attr", [P, BLK, 2 * P])
        attr_one = sb("attr_one", [P, 2, BLK, P])
        dst = sb("dst", [P, BLK, P])
        nxt = sb("nxt", [P, BLK, P])
        src = sb("src", [P, BLK, P])
        firsts = sb("firsts", [P, BLK, P])
        first_row = sb("first_row", [P, COLS])
        node0 = sb("node0", [P, 2, BLK])
        tile_no = sb("tile_no", [P, BLK])
        below = sb("below", [P, BLK, COLS])
        cnt = sb("cnt", [P, 2, BLK])
        need = sb("need", [P, PAIRS, BLK])
        need_idx = sb("need_idx", [P, PAIRS, BLK], I32)
        lap = sb("lap", [P, PAIRS, BLK])
        packed = sb("packed", [P, 2, BLK, 4])
        bad = sb("bad", [P, 3])
        next0, span, lead, live, wide, far, near = (
            sb(n, [P, BLK]) for n in ("next0", "span", "lead", "live", "wide", "far", "near"))
        needed = sb("needed", [P, PAIRS, BLK, P])
        slots = sb("slots", [1, 2, COLS * 4])
        any_third = sb("any_third", [1, COLS // 4])
        slow = sb("slow", [1, 1])
        w_nat = [sb(f"w_nat{i}", [P, D]) for i in range(2)]
        wl_nat = sb("wl_nat", [P, 2 * D])
        b_col = sb("b_col", [P, 2])
        squares = sb("squares", [P, 2, D])
        b_sum, b_clamp, b_inv, b_norm, b_tanh, b_scale = (
            sb(n, [P, 2]) for n in ("b_sum", "b_clamp", "b_inv", "b_norm", "b_tanh", "b_scale"))

        zeroed = sem("zeroed")
        loaded = sem("loaded")
        consts = sem("consts")
        dst_ready = sem("dst_ready")
        firsts_ready = sem("firsts_ready")
        first_ps = sem("first_ps")
        need_ready = sem("need_ready")
        rows_out = sem("rows_out")
        gathered = sem("gathered")
        slots_ready = sem("slots_ready")
        slots_out = sem("slots_out")
        slots_in = sem("slots_in")
        cols_ps = sem("cols_ps")
        cols_out = sem("cols_out")
        w_ps = sem("w_ps")
        rel_ready = sem("rel_ready")
        rel_ps = sem("rel_ps")
        b_norm_ready = sem("b_norm_ready")
        b_tanh_ready = sem("b_tanh_ready")
        b_col_ready = sem("b_col_ready")
        end_ps = sem("end_ps")
        dve_chain = sem("dve_chain")
        pool_chain = sem("pool_chain")

        whole = (BLK - 1) * P * P
        rest = (ET - 1) - (BLK - 1) * P
        rows_end = whole + rest * P

        with nc.Block() as block:
            @block.sync
            def _(sp):
                sp.wait_ge(zeroed, 5)
                lists = ((io["dst"], dst_int, 1, 0), (io["dst"], next_int, 1, 1), (io["src"], src_int, 1, 0),
                         (io["edge_weight"], weight, 1, 0), (io["edge_attr_2"].rearrange("e c -> (e c)"), attr, 2, 0))
                for vec, to, w, shift in lists:
                    a, b, end = shift + w * whole, shift + w * rows_end, w * E
                    sp.dma_start(to[:, 0:BLK - 1, :],
                                 vec[shift:a].rearrange("(b r l) -> r b l", r=P, l=w * P)).then_inc(loaded, 16)
                    sp.dma_start(to[0:rest, BLK - 1, :],
                                 vec[a:b].rearrange("(r l) -> r l", l=w * P)).then_inc(loaded, 16)
                    sp.dma_start(to[rest:rest + 1, BLK - 1, 0:end - b],
                                 vec[b:end].rearrange("(r l) -> r l", r=1)).then_inc(loaded, 16)
                for i, (w, bv) in enumerate(((io["W1"], io["b1"]), (io["W2"], io["b2"]))):
                    sp.dma_start(w_nat[i][:, :], w).then_inc(loaded, 16)
                    sp.dma_start(c.bias[i][:, :], bv.partition_broadcast(P)).then_inc(loaded, 16)
                    sp.dma_start(b_col[:, i:i + 1], bv.rearrange("(o u) -> o u", u=1)).then_inc(loaded, 16)
                sp.dma_start(wl_nat[:, :], io["W"]).then_inc(loaded, 16)
                sp.dma_start(c.b_l1[:, :], io["b"].partition_broadcast(P)).then_inc(loaded, 16)
                sp.wait_ge(dst_ready, 1)
                sp.dma_start(dram["dst_rows"].rearrange("(b r) l -> r b l", r=P), dst[:, :, :]).then_inc(rows_out, 16)
                sp.wait_ge(slots_ready, 1)
                for k in range(2):
                    sp.dma_start(dram["slots"][k].rearrange("(b r j) -> r b j", r=P, j=4),
                                 packed[:, k]).then_inc(slots_out, 16)
                sp.wait_ge(slots_out, 32)
                sp.dma_start(slots[0:1, :, :], dram["slots"].rearrange("(u k) n -> u k n", u=1)).then_inc(slots_in, 16)
                sp.wait_ge(slots_in, 16)

            loads = 15 + 8

            @block.gpsimd
            def _(pool):
                g = nc.gpsimd
                g.memset(dst_int[:, :, :], int(PAD_DST)).then_inc(zeroed, 1)
                g.memset(next_int[:, :, :], int(PAD_DST)).then_inc(zeroed, 1)
                g.memset(src_int[:, :, :], 0).then_inc(zeroed, 1)
                g.memset(weight[:, :, :], 0.0).then_inc(zeroed, 1)
                g.memset(attr[:, :, :], 0.0).then_inc(zeroed, 1)
                g.memset(c.zeros[:, :], 0.0)
                g.memset(c.zero_row[:, :], 0.0)
                g.memset(c.ones[:, :], 1.0).then_inc(pool_chain, 1)
                pool.wait_ge(pool_chain, 1)
                small = dict(allow_small_or_imprecise_dtypes=True)
                g.iota(c.iota_row[:, :], pattern=[[1, P]], base=0, channel_multiplier=0, **small)
                g.iota(c.trash[:, :], pattern=[[1, 1]], base=ROWS, channel_multiplier=1, **small)
                for j in range(2):
                    g.iota(node0[:, j, :], pattern=[[P * P, BLK]], base=P * j, channel_multiplier=P, **small)
                g.iota(tile_no[:, :], pattern=[[P, BLK]], base=0, channel_multiplier=1, **small)
                g.affine_select(out=c.ident[:, :], in_=c.ones[:, :], compare_op=ALU.is_equal, fill=0.0, base=0,
                                pattern=[[-1, P]], channel_multiplier=1)
                g.affine_select(out=c.earlier[:, :], in_=c.ones[:, :], compare_op=ALU.is_gt, fill=0.0, base=0,
                                pattern=[[-1, P]], channel_multiplier=1).then_inc(consts, 1)
                pool.wait_ge(need_ready, 1)
                pool.wait_ge(rows_out, 16)
                for j in range(PAIRS):
                    for b in range(BLK):
                        g.indirect_dma_start(out=needed[:, j, b, :], out_offset=None, in_=dram["dst_rows"],
                                             in_offset=bass.IndirectOffsetOnAxis(ap=need_idx[:, j, b:b + 1].bitcast(U32), axis=0)
                                             ).then_inc(gathered, 16)

            @block.tensor
            def _(pe):
                pe.wait_ge(consts, 1)
                pe.wait_ge(loaded, 16 * loads)
                pe.wait_ge(firsts_ready, 1)
                for b in range(BLK):
                    last = pe.matmul(bank[0][:, b * P:(b + 1) * P], c.ones[:, :], firsts[:, b, :], start=True, stop=True)
                last.then_inc(first_ps, 1)
                for n, have in enumerate((src, weight, attr_one[:, 0], attr_one[:, 1], dst)):
                    for b in range(BLK):
                        last = pe.transpose(bank[1 + n][:, b * P:(b + 1) * P], have[:, b, :], c.ident[:, :])
                last.then_inc(cols_ps, 1)
                for i in range(2):
                    pe.transpose(bank[6][:, i * P:(i + 1) * P], w_nat[i][:, :], c.ident[:, :])
                for i in range(2):
                    last = pe.transpose(bank[6][:, (2 + i) * P:(3 + i) * P], wl_nat[:, i * D:(i + 1) * D], c.ident[:, :])
                last.then_inc(w_ps, 1)
                pe.wait_ge(rel_ready, 1)
                pe.wait_ge(cols_out, 1)
                for j in range(PAIRS):
                    for b in range(BLK):
                        last = pe.transpose(bank[1 + j][:, b * P:(b + 1) * P], needed[:, j, b, :], c.ident[:, :])
                last.then_inc(rel_ps, 1)
                pe.wait_ge(b_col_ready, 1)
                for i in range(2):
                    pe.matmul(bank[7][:, i:i + 1], w_nat[i][:, :], b_col[:, i:i + 1], start=True, stop=True)
                pe.matmul(bank[7][0:1, 4:5], bad[:, 2:3], c.ones[:, 0:1], start=True, stop=True).then_inc(end_ps, 1)

            @block.scalar
            def _(act):
                act.wait_ge(b_norm_ready, 1)
                act.activation(b_tanh[:, :], b_norm[:, :], ACT.Tanh).then_inc(b_tanh_ready, 1)

            @block.vector
            def _(dve):
                v = nc.vector
                link = Chain(dve, dve_chain, 0)
                dve.wait_ge(consts, 1)
                dve.wait_ge(loaded, 16 * loads)
                v.tensor_copy(nxt[:, :, :], next_int[:, :, :])
                v.tensor_copy(src[:, :, :], src_int[:, :, :])
                for i in range(2):
                    v.tensor_copy(attr_one[:, i], attr[:, :, :].rearrange("p b (l a) -> p b l a", a=2)[:, :, :, i])
                link(v.tensor_copy(dst[:, :, :], dst_int[:, :, :]))
                dve.sem_inc(dst_ready, 1)
                link(v.tensor_tensor(firsts[:, :, :], under(c.ident[:, :], BLK), over(dst[:, :, 0], P), ALU.mult))
                dve.sem_inc(firsts_ready, 1)
                link(v.tensor_tensor(nxt[:, :, :], dst[:, :, :], nxt[:, :, :], ALU.is_gt))
                link(v.tensor_reduce(bad[:, 0:1], nxt[:, :, :].rearrange("p b l -> p (b l)"), X, ALU.add))
                dve.wait_ge(first_ps, 1)
                link(v.tensor_copy(first_row[:, :], bank[0][:, :]))
                for j in range(2):
                    link(v.tensor_tensor(below[:, :, :], under(first_row[:, :], BLK), over(node0[:, j, :], COLS), ALU.is_lt))
                    link(v.tensor_reduce(cnt[:, j, :], below[:, :, :], X, ALU.add))
                need0 = need[:, 0, :]
                v.tensor_scalar(need0, cnt[:, 0, :], -1.0, 0.0, ALU.add, ALU.max)
                link(v.tensor_scalar(next0[:, :], cnt[:, 1, :], -1.0, 0.0, ALU.add, ALU.max))
                for j in range(1, PAIRS):
                    v.tensor_scalar(need[:, j, :], need0, float(j), float(COLS - 1), ALU.add, ALU.min)
                v.tensor_tensor(span[:, :], next0[:, :], need0, ALU.subtract)
                link(v.tensor_tensor(lead[:, :], need0, tile_no[:, :], ALU.subtract))
                link(v.tensor_copy(need_idx[:, :, :], need[:, :, :]))
                dve.sem_inc(need_ready, 1)
                lap_of = float(4 * RING)
                link(v.tensor_scalar(lap[:, :, :], need[:, :, :], lap_of, None, ALU.is_ge))
                for k in range(2, COLS // (4 * RING) + 1):
                    link(v.scalar_tensor_tensor(out=lap[:, :, :], in0=need[:, :, :], scalar=lap_of * k,
                                                in1=lap[:, :, :], op0=ALU.is_ge, op1=ALU.add))
                link(v.scalar_tensor_tensor(out=lap[:, :, :], in0=lap[:, :, :], scalar=-lap_of,
                                            in1=need[:, :, :], op0=ALU.mult, op1=ALU.add))
                for k in range(2):
                    v.tensor_scalar(packed[:, k, :, 0:PAIRS], lap[:, :, :].rearrange("p j b -> p b j"),
                                    float(D * (k + 1)), None, ALU.mult)
                    last = v.tensor_scalar(packed[:, k, :, PAIRS], span[:, :], float(PAIRS - 1), None, ALU.is_ge)
                link(last)
                dve.sem_inc(slots_ready, 1)
                for i in range(2):
                    last = v.tensor_tensor(squares[:, i, :], c.bias[i][:, :], c.bias[i][:, :], ALU.mult)
                link(last)
                link(v.tensor_reduce(b_sum[:, :], squares[:, :, :], X, ALU.add))
                link(v.tensor_scalar(b_clamp[:, :], b_sum[:, :], TINY, None, ALU.max))
                inverse_root(v, link, b_inv[:, :], b_clamp[:, :], b_norm[:, :])
                v.tensor_scalar(live[:, :], tile_no[:, :], float(4 * NQ), None, ALU.is_lt)
                v.tensor_scalar(wide[:, :], span[:, :], float(PAIRS), None, ALU.is_ge)
                v.tensor_scalar(far[:, :], lead[:, :], float(4 * AHEAD - PAIRS + 1), None, ALU.is_gt)
                link(v.tensor_scalar(near[:, :], lead[:, :], float(-BEHIND), None, ALU.is_lt))
                link(v.tensor_tensor(wide[:, :], wide[:, :], far[:, :], ALU.add))
                link(v.tensor_tensor(wide[:, :], wide[:, :], near[:, :], ALU.add))
                link(v.tensor_tensor(wide[:, :], wide[:, :], live[:, :], ALU.mult))
                link(v.tensor_reduce(bad[:, 1:2], wide[:, :], X, ALU.add))
                link(v.tensor_tensor(bad[:, 2:3], bad[:, 0:1], bad[:, 1:2], ALU.add))
                dve.wait_ge(cols_ps, 1)
                for n, to in enumerate((c.src_col, c.weight_col, c.attr_col[0], c.attr_col[1], c.dst_col)):
                    last = v.tensor_copy(to[:, :], bank[1 + n][:, :])
                link(last)
                dve.sem_inc(cols_out, 1)
                dve.wait_ge(w_ps, 1)
                for i in range(2):
                    v.tensor_copy(c.w_t[i][:, 0:D], bank[6][:, i * P:(i + 1) * P])
                v.tensor_copy(c.w_l1[:, :], bank[6][:, 2 * P:4 * P])
                dve.wait_ge(gathered, 16 * PAIRS * BLK)
                for j in range(PAIRS):
                    last = v.tensor_tensor(needed[:, j], needed[:, j], over(node0[:, 0, :], P), ALU.subtract)
                link(last)
                dve.sem_inc(rel_ready, 1)
                link(v.tensor_tensor(b_norm[:, :], b_clamp[:, :], b_inv[:, :], ALU.mult))
                dve.sem_inc(b_norm_ready, 1)
                dve.wait_ge(b_tanh_ready, 1)
                link(v.tensor_scalar(b_tanh[:, :], b_tanh[:, :], BALL, None, ALU.min))
                link(v.tensor_tensor(b_scale[:, :], b_tanh[:, :], b_inv[:, :], ALU.mult))
                link(v.tensor_tensor(b_sum[:, :], b_sum[:, :], b_scale[:, :], ALU.mult))
                link(v.tensor_tensor(b_sum[:, :], b_sum[:, :], b_scale[:, :], ALU.mult))
                for i in range(2):
                    v.tensor_scalar(c.bias[i][:, :], c.bias[i][:, :], b_scale[:, i:i + 1], None, ALU.mult)
                    v.tensor_copy(c.y2[i][:, :], b_sum[:, i:i + 1])
                    v.tensor_scalar(c.y2p1[i][:, :], b_sum[:, i:i + 1], 1.0, None, ALU.add)
                link(v.tensor_tensor(b_col[:, :], b_col[:, :], b_scale[:, :], ALU.mult))
                dve.sem_inc(b_col_ready, 1)
                dve.wait_ge(rel_ps, 1)
                for j in range(PAIRS):
                    v.tensor_copy(c.dst_in_tile[:, :, j], bank[1 + j][:, :])
                dve.wait_ge(end_ps, 1)
                for i in range(2):
                    v.tensor_copy(c.w_t[i][:, D:D + 1], bank[7][:, i:i + 1])
                link(v.tensor_scalar(slow[:, :], bank[7][0:1, 4:5], 0.0, None, ALU.is_gt))
                link(v.tensor_copy(c.slow[:, :], slow[:, :]))
                dve.wait_ge(slots_in, 16)
                for k, row in enumerate((c.slot_row, c.slot_row_wide)):
                    by_quad = slots[:, k, :].rearrange("p (m r j) -> p m r j", r=4, j=4)
                    v.tensor_copy(row[:, :, 0:8].rearrange("p m (r j) -> p m r j", j=2), by_quad[:, :, :, 0:2])
                    v.tensor_copy(row[:, :, 9:13], by_quad[:, :, :, 2])
                    link(v.tensor_reduce(any_third[:, :], by_quad[:, :, :, PAIRS], X, ALU.max))
                    link(v.tensor_copy(row[:, :, 8], any_third[:, :]))


def hyper_pass(nc, c, name, layer, source, table, normed):
    with semaphores(nc, name) as sem, ExitStack() as ctx:
        def sb(n, shape, dtype=F32):
            return ctx.enter_context(nc.sbuf_tensor(f"{name}_{n}", shape, dtype))

        def banks(n, k):
            return [ctx.enter_context(nc.psum_tensor(f"{name}_{n}{i}", [P, 512], F32)) for i in range(k)]

        rows = [sb(f"rows{i}", [P, GT * D]) for i in range(2)]
        prod = [sb(f"prod{i}", [P, GT * D]) for i in range(2)]
        made = sb("made", [P, GT * D])
        row_sq = [sb(f"row_sq{i}", [P, GT * D]) for i in range(2)]
        prod_sq = sb("prod_sq", [P, GT * D])
        bias_part = sb("bias_part", [P, GT * D])
        turned = [sb(f"turned{i}", [P, 4 * P]) for i in range(2)]
        turn_ps = banks("turn_ps", 2)
        prod_ps = [ctx.enter_context(nc.psum_tensor(f"{name}_prod_ps{i}", [P, 2, 512], F32)) for i in range(2)]
        qb_raw = [sb(f"qb_raw{i}", [P, GT]) for i in range(2)]
        stats = sb("stats", [P, GT, 6])
        mean, var, gap = (sb(n, [P, GT]) for n in ("mean", "var", "gap"))
        roots, inv_roots, newton = (sb(n, [P, 3, GT]) for n in ("roots", "inv_roots", "newton"))
        dev = [sb(f"dev{i}", [P, GT]) for i in range(2)]
        qsum = [sb(f"qsum{i}", [P, GT]) for i in range(2)]
        (inv_dev2, qb, clip, arg, th, mag, dirn, xy2, mag2, pn, den, al, be, n2, t1, t2, inv_n, nn, up, down,
         ratio, log, z, poly, small, f) = (sb(n, [P, GT]) for n in (
             "inv_dev2", "qb", "clip", "arg", "th", "mag", "dirn", "xy2", "mag2", "pn", "den", "al", "be", "n2",
             "t1", "t2", "inv_n", "nn", "up", "down", "ratio", "log", "z", "poly", "small", "f"))

        loaded = [sem(f"loaded{i}") for i in range(2)]
        tail_loaded = sem("tail_loaded")
        centred = sem("centred")
        turned_ps = sem("turned_ps")
        relued = sem("relued")
        multiplied = sem("multiplied")
        copied = sem("copied")
        lifted = sem("lifted")
        squared = sem("squared")
        squared_too = sem("squared_too")
        summed = sem("summed")
        tanh_in, tanh_out = sem("tanh_in"), sem("tanh_out")
        log_in, log_out = sem("log_in"), sem("log_out")
        factors = sem("factors")
        scaled = sem("scaled")
        biased = sem("biased")
        finished = sem("finished")
        stored = sem("stored")
        dve_chain = sem("dve_chain")

        POOL_SQ = GQ if normed else 4

        has_tail = source.shape[0] < ROWS

        def quad(buf, k):
            return buf[:, 4 * D * k:4 * D * (k + 1)]

        def cols(buf, k):
            return buf[:, 4 * k:4 * (k + 1)]

        with nc.Block() as block:

            @block.sync
            def _(sp):
                def load(i, par):
                    if not (isinstance(i, int) and i < 2):
                        sp.wait_ge(turned_ps, GQ * (i - 1))
                        if normed:
                            sp.wait_ge(lifted, GQ * (i - 1))
                        else:
                            sp.wait_ge(squared, GQ * (i - 1))
                            sp.wait_ge(squared_too, GQ * (i - 1))
                    if has_tail and isinstance(i, int) and i == NGRP - 1:
                        first = GT * P * i
                        whole, some = divmod(N - first, GT)
                        sp.dma_start(rows[par][whole:whole + 1, 0:some * D], source[first + whole * GT:N, :].rearrange(
                            "(p t) d -> p (t d)", p=1)).then_inc(tail_loaded, 16)
                        sp.wait_ge(tail_loaded, 16)
                        sp.dma_start(rows[par][0:whole, :], source[first:first + whole * GT, :].rearrange(
                            "(p t) d -> p (t d)", t=GT)).then_inc(loaded[par], 16)
                    else:
                        sp.dma_start(rows[par][:, :], source[bass.ds(GT * P * i, GT * P), :].rearrange(
                            "(p t) d -> p (t d)", t=GT)).then_inc(loaded[par], 16)

                def store(i):
                    sp.wait_ge(finished, GQ * (i + 1))
                    sp.dma_start(table[bass.ds(GT * P * i, GT * P), :].rearrange("(p t) d -> p (t d)", t=GT),
                                 made[:, :]).then_inc(stored, 16)

                def step(h, par, first=False):
                    load(2 * h + (2 + par), par)
                    if not first:
                        store(2 * h + par - 1)

                load(0, 0)
                load(1, 1)
                for par in range(2):
                    step(0, par, par == 0)
                with sp.Fori(1, NGRP // 2 - 2) as h:
                    for par in range(2):
                        step(h, par)
                for par in range(2):
                    step(NGRP // 2 - 2, par)
                for i in range(NGRP - 3, NGRP):
                    store(i)
                sp.wait_ge(stored, 16 * NGRP)

            @block.gpsimd
            def _(pool):
                g = nc.gpsimd

                def squares(h, par):
                    i = 2 * h + par
                    if not normed:
                        pool.wait_ge(loaded[par], 16 * (h + 1))
                        at_least(pool, summed, i - 1)
                    for k in range(POOL_SQ):
                        if normed:
                            pool.wait_ge(lifted, GQ * i + k + 1)
                        have = row_sq[par] if normed else rows[par]
                        g.tensor_tensor(quad(row_sq[par], k), quad(have, k), quad(have, k), ALU.mult).then_inc(
                            squared, GQ - POOL_SQ + 1 if k == POOL_SQ - 1 else 1)

                def bias_parts(i, par):
                    pool.wait_ge(factors, i + 1)
                    at_least(pool, finished, GQ * i)
                    for k in range(GQ):
                        g.tensor_tensor(tiles(quad(bias_part, k)), under(c.bias[layer][:, :], 4), over(cols(be, k), D),
                                        ALU.mult).then_inc(biased, 1)
                    for k in range(GQ):
                        pool.wait_ge(scaled, GQ * i + k + 1)
                        pool.wait_ge(biased, GQ * i + k + 1)
                        g.tensor_tensor(quad(made, k), quad(made, k), quad(bias_part, k), ALU.add).then_inc(finished, 1)

                def step(h, par):
                    i = 2 * h + par
                    squares(h, par)
                    if not (isinstance(i, int) and i == 0):
                        bias_parts(i - 1, 1 - par)

                for par in range(2):
                    step(0, par)
                with pool.Fori(1, NGRP // 2) as h:
                    for par in range(2):
                        step(h, par)
                bias_parts(NGRP - 1, (NGRP - 1) % 2)

            @block.tensor
            def _(pe):
                def turn(h, par, k):
                    q = GQ * (2 * h + par) + k
                    if normed:
                        pe.wait_ge(centred, q + 1)
                    elif k == 0:
                        pe.wait_ge(loaded[par], 16 * (h + 1))
                    at_least(pe, relued, q - 1)
                    for r in range(4):
                        last = pe.transpose(turn_ps[(k + par) % 2][:, r * P:(r + 1) * P],
                                            rows[par][:, (4 * k + r) * D:(4 * k + r + 1) * D], c.ident[:, :])
                    last.then_inc(turned_ps, 1)

                def multiply(h, par, k):
                    i = 2 * h + par
                    q = GQ * i + k
                    slot = (k + par) % 2
                    pe.wait_ge(relued, q + 1)
                    at_least(pe, copied, q - 1)
                    for r in range(4):
                        r_t = turned[slot][:, r * P:(r + 1) * P]
                        last = pe.matmul(prod_ps[slot][:, r // 2, (r % 2) * (D + 1):(r % 2 + 1) * (D + 1)], r_t,
                                         c.w_t[layer][:, :], start=True, stop=True)
                    last.then_inc(multiplied, 1)

                def step(h, par):
                    for k in range(GQ):
                        turn(h, par, k)
                        if k:
                            multiply(h, par, k - 1)
                    multiply(h, par, GQ - 1)

                for par in range(2):
                    step(0, par)
                with pe.Fori(1, NGRP // 2) as h:
                    for par in range(2):
                        step(h, par)

            @block.scalar
            def _(act):
                TANH_AT, LOG_AT = 2, GQ - 2

                def take_turned(h, par, k):
                    q = GQ * (2 * h + par) + k
                    slot = (k + par) % 2
                    act.wait_ge(turned_ps, q + 1)
                    at_least(act, multiplied, q - 1)
                    act.activation(turned[slot][:, :], turn_ps[slot][:, :], ACT.Relu).then_inc(relued, 1)

                def lift(h, par, k):
                    i = 2 * h + par
                    if k == 0:
                        at_least(act, summed, i - 1)
                    act.wait_ge(centred, GQ * i + k + 1)
                    act.activation(quad(row_sq[par], k), quad(rows[par], k), ACT.Relu).then_inc(lifted, 1)

                def square(h, par, k):
                    if k == POOL_SQ:
                        act.wait_ge(loaded[par], 16 * (h + 1))
                        at_least(act, summed, 2 * h + par - 1)
                    act.activation(quad(row_sq[par], k), quad(rows[par], k), ACT.Square).then_inc(
                        squared_too, POOL_SQ + 1 if k == GQ - 1 else 1)

                def take_product(h, par, k):
                    i = 2 * h + par
                    q = GQ * i + k
                    slot = (k + par) % 2
                    act.wait_ge(multiplied, q + 1)
                    if k == 0:
                        at_least(act, scaled, GQ * (i - 1))
                    both = prod_ps[slot][:, :, 0:2 * (D + 1)].rearrange("p a (b d) -> p a b d", b=2)
                    act.activation(quad(prod[par], k).rearrange("p (a b d) -> p a b d", a=2, b=2), both[:, :, :, 0:D], ACT.Copy)
                    act.activation(cols(qb_raw[par], k).rearrange("p (a b u) -> p a b u", a=2, u=1), both[:, :, :, D:D + 1], ACT.Copy)
                    for r in range(4):
                        t = 4 * k + r
                        last = act.activation(prod_sq[:, t * D:(t + 1) * D], both[:, r // 2, r % 2, 0:D],
                                              ACT.Square, accum_out=qsum[par][:, t:t + 1])
                    last.then_inc(copied, 1)

                def tanh(i):
                    act.wait_ge(tanh_in, i + 1)
                    act.activation(th[:, :], arg[:, :], ACT.Tanh).then_inc(tanh_out, 1)

                def logarithm(i):
                    act.wait_ge(log_in, i + 1)
                    act.activation(log[:, :], ratio[:, :], ACT.Ln).then_inc(log_out, 1)

                def step(h, par):
                    i = 2 * h + par
                    first = isinstance(i, int) and i == 0
                    for k in range(GQ):
                        if normed:
                            lift(h, par, k)
                        take_turned(h, par, k)
                        if k >= POOL_SQ:
                            square(h, par, k)
                        if k:
                            take_product(h, par, k - 1)
                        if k == TANH_AT and not first:
                            tanh(i - 1)
                        if k == LOG_AT and not first:
                            logarithm(i - 1)
                    take_product(h, par, GQ - 1)

                for par in range(2):
                    step(0, par)
                with act.Fori(1, NGRP // 2) as h:
                    for par in range(2):
                        step(h, par)
                tanh(NGRP - 1)
                logarithm(NGRP - 1)

            @block.vector
            def _(dve):
                v = nc.vector

                def stats_of(h, par, t):
                    if t == 0:
                        dve.wait_ge(loaded[par], 16 * (h + 1))
                    return v.bn_stats(stats[:, t, :], rows[par][:, t * D:(t + 1) * D])

                def centre(h, par, link):
                    x = tiles(rows[par][:, :])
                    link(v.tensor_tensor(mean[:, :], stats[:, :, 1], stats[:, :, 4], ALU.add))
                    link(v.tensor_scalar(mean[:, :], mean[:, :], 0.5, None, ALU.mult))

                    def centre_quad(k):
                        v.tensor_tensor(x[:, 4 * k:4 * k + 4, :], x[:, 4 * k:4 * k + 4, :],
                                        over(cols(mean, k), D), ALU.subtract).then_inc(centred, 1)

                    centre_quad(0)
                    link.beside(lambda n: centre_quad(n + 1))
                    v.tensor_tensor(gap[:, :], stats[:, :, 1], stats[:, :, 4], ALU.subtract)
                    link(v.tensor_tensor(var[:, :], stats[:, :, 2], stats[:, :, 5], ALU.add))
                    link(v.tensor_tensor(gap[:, :], gap[:, :], gap[:, :], ALU.mult))
                    link(v.tensor_scalar(var[:, :], var[:, :], 1.0 / D, 1e-5, ALU.mult, ALU.add))
                    link(v.scalar_tensor_tensor(out=dev[par][:, :], in0=gap[:, :], scalar=0.25, in1=var[:, :],
                                                op0=ALU.mult, op1=ALU.add))
                    link.beside(None)
                    for k in range(5, GQ):
                        centre_quad(k)

                S, Q = roots[:, 0, :], roots[:, 1, :]
                inv_s, inv_q, inv_dev = inv_roots[:, 0, :], inv_roots[:, 1, :], inv_roots[:, 2, :]
                nroots = 3 if normed else 2

                def rapidity(i, par, link):
                    dve.wait_ge(squared, GQ * (i + 1))
                    if POOL_SQ < GQ:
                        dve.wait_ge(squared_too, GQ * (i + 1))
                    link(v.tensor_reduce(S, tiles(row_sq[par][:, :]), X, ALU.add))
                    dve.sem_inc(summed, 1)
                    dve.wait_ge(copied, GQ * (i + 1))
                    link(v.tensor_copy(Q, qsum[par][:, :]))
                    if normed:
                        v.tensor_copy(roots[:, 2, :], dev[par][:, :])
                        link(v.reciprocal(inv_dev2[:, :], dev[par][:, :]))
                        link(v.tensor_tensor(roots[:, 0:2, :], roots[:, 0:2, :], under(inv_dev2[:, :], 2), ALU.mult))
                    link(v.tensor_scalar(roots[:, 0:nroots, :], roots[:, 0:nroots, :], TINY, None, ALU.max))
                    inverse_root(v, link, inv_roots[:, 0:nroots, :], roots[:, 0:nroots, :], newton[:, 0:nroots, :])
                    if normed:
                        v.tensor_tensor(qb[:, :], qb_raw[par][:, :], inv_dev, ALU.mult)
                    else:
                        v.tensor_copy(qb[:, :], qb_raw[par][:, :])
                    v.tensor_scalar(clip[:, :], inv_s, ATANH_MAX, 1.0, ALU.mult, ALU.min)
                    link(v.tensor_tensor(arg[:, :], Q, inv_q, ALU.mult))
                    link(v.tensor_tensor(arg[:, :], arg[:, :], clip[:, :], ALU.mult))
                    dve.sem_inc(tanh_in, 1)

                def factor(i, par, link, beside_log=None):
                    dve.wait_ge(tanh_out, i + 1)
                    at_least(dve, biased, GQ * i)
                    link(v.tensor_scalar(mag[:, :], th[:, :], BALL, None, ALU.min))
                    v.tensor_tensor(mag2[:, :], mag[:, :], mag[:, :], ALU.mult)
                    link(v.tensor_tensor(dirn[:, :], mag[:, :], inv_q, ALU.mult))
                    link(v.scalar_tensor_tensor(out=xy2[:, :], in0=dirn[:, :], scalar=2.0, in1=qb[:, :], op0=ALU.mult, op1=ALU.mult))
                    v.tensor_scalar(pn[:, :], xy2[:, :], c.y2p1[layer][:, :], None, ALU.add)
                    v.scalar_tensor_tensor(out=den[:, :], in0=mag2[:, :], scalar=c.y2[layer][:, :], in1=xy2[:, :],
                                           op0=ALU.mult, op1=ALU.add)
                    link(v.tensor_scalar(be[:, :], mag2[:, :], -1.0, 1.0, ALU.mult, ALU.add))
                    v.tensor_tensor(al[:, :], pn[:, :], dirn[:, :], ALU.mult)
                    link(v.tensor_scalar(den[:, :], den[:, :], 1.0, 1e-15, ALU.add, ALU.max))
                    link(v.reciprocal(den[:, :], den[:, :]))
                    v.tensor_tensor(al[:, :], al[:, :], den[:, :], ALU.mult)
                    link(v.tensor_tensor(be[:, :], be[:, :], den[:, :], ALU.mult))
                    v.tensor_tensor(t1[:, :], al[:, :], al[:, :], ALU.mult)
                    v.tensor_tensor(t2[:, :], al[:, :], qb[:, :], ALU.mult)
                    link(v.tensor_scalar(n2[:, :], be[:, :], c.y2[layer][:, :], None, ALU.mult))
                    v.tensor_tensor(t1[:, :], t1[:, :], Q, ALU.mult)
                    link(v.scalar_tensor_tensor(out=t2[:, :], in0=t2[:, :], scalar=2.0, in1=n2[:, :], op0=ALU.mult, op1=ALU.add))
                    link(v.tensor_tensor(t2[:, :], t2[:, :], be[:, :], ALU.mult))
                    link(v.tensor_tensor(n2[:, :], t1[:, :], t2[:, :], ALU.add))
                    link(v.tensor_scalar(n2[:, :], n2[:, :], TINY, None, ALU.max))
                    inverse_root(v, link, inv_n[:, :], n2[:, :], t1[:, :])
                    link(v.tensor_tensor(nn[:, :], n2[:, :], inv_n[:, :], ALU.mult))
                    link(v.tensor_scalar(nn[:, :], nn[:, :], BALL, None, ALU.min))
                    v.tensor_scalar(up[:, :], nn[:, :], 1.0, None, ALU.add)
                    link(v.tensor_scalar(down[:, :], nn[:, :], -1.0, 1.0, ALU.mult, ALU.add))
                    link(v.reciprocal(down[:, :], down[:, :]))
                    link(v.tensor_tensor(ratio[:, :], up[:, :], down[:, :], ALU.mult))
                    dve.sem_inc(log_in, 1)
                    link.beside(None)
                    if beside_log is not None:
                        beside_log()
                    v.tensor_scalar(small[:, :], nn[:, :], SMALL, None, ALU.is_lt)
                    link(v.tensor_tensor(z[:, :], nn[:, :], nn[:, :], ALU.mult))
                    link(v.tensor_scalar(poly[:, :], z[:, :], 1.0 / 9, 1.0 / 7, ALU.mult, ALU.add))
                    link(v.tensor_tensor(poly[:, :], poly[:, :], z[:, :], ALU.mult))
                    link(v.scalar_tensor_tensor(out=poly[:, :], in0=poly[:, :], scalar=1.0 / 5, in1=z[:, :], op0=ALU.add, op1=ALU.mult))
                    link(v.scalar_tensor_tensor(out=poly[:, :], in0=poly[:, :], scalar=1.0 / 3, in1=z[:, :], op0=ALU.add, op1=ALU.mult))
                    link(v.scalar_tensor_tensor(out=poly[:, :], in0=poly[:, :], scalar=1.0, in1=nn[:, :], op0=ALU.add, op1=ALU.mult))
                    dve.wait_ge(log_out, i + 1)
                    link(v.scalar_tensor_tensor(out=poly[:, :], in0=log[:, :], scalar=-0.5, in1=poly[:, :], op0=ALU.mult, op1=ALU.add))
                    link(v.tensor_tensor(poly[:, :], poly[:, :], small[:, :], ALU.mult))
                    link(v.scalar_tensor_tensor(out=f[:, :], in0=log[:, :], scalar=0.5, in1=poly[:, :], op0=ALU.mult, op1=ALU.add))
                    link(v.tensor_tensor(f[:, :], f[:, :], inv_n[:, :], ALU.mult))
                    v.tensor_tensor(be[:, :], be[:, :], f[:, :], ALU.mult)
                    link(v.tensor_tensor(al[:, :], al[:, :], f[:, :], ALU.mult))
                    if normed:
                        link(v.tensor_tensor(al[:, :], al[:, :], inv_dev, ALU.mult))
                    dve.sem_inc(factors, 1)

                def scale(i, par):
                    at_least(dve, stored, 16 * i)
                    for k in range(GQ):
                        v.tensor_tensor(tiles(quad(made, k)), tiles(quad(prod[par], k)), over(cols(al, k), D),
                                        ALU.mult).then_inc(scaled, 1)

                first_links = 14 if normed else 0
                links = LINKS[normed]

                def step(h, par, more, start=None):
                    i = 2 * h + par
                    link = Chain(dve, dve_chain, first_links + i * links if start is None else start)
                    rapidity(i, par, link)
                    if normed and more:
                        def statistics(n):
                            for t in range(2 * n, 2 * n + 2) if n < 2 else range(n + 2, min(n + 3, GT)):
                                stats_of(h + 1, par, t)

                        link.beside(statistics)
                        factor(i, par, link, lambda: centre(h + 1, par, link))
                    else:
                        factor(i, par, link)
                    scale(i, par)
                    return link.count

                if normed:
                    link = Chain(dve, dve_chain, 0)
                    for par in range(2):
                        for t in range(GT):
                            last = stats_of(0, par, t)
                        link(last)
                        centre(0, par, link)
                    assert link.count == first_links, link.count
                count = step(0, 0, True)
                assert count == first_links + links, count - first_links
                step(0, 1, True)
                with dve.Fori(1, NGRP // 2 - 1) as h:
                    for par in range(2):
                        step(h, par, True)
                count = None
                for par in range(2):
                    count = step(NGRP // 2 - 1, par, False, count)


LINKS = {True: 62, False: 53}
RESIDUAL_LINKS = 29


def residual_pass(nc, c, name, sums, x, x2, table):
    with semaphores(nc, name) as sem, ExitStack() as ctx:
        def sb(n, shape, dtype=F32):
            return ctx.enter_context(nc.sbuf_tensor(f"{name}_{n}", shape, dtype))

        rows = [sb(f"rows{i}", [P, GT * D]) for i in range(2)]
        fresh = sb("fresh", [P, GT * D])
        resid = [sb(f"resid{i}", [P, GT * D]) for i in range(2)]
        row_sq = [sb(f"row_sq{i}", [P, GT * D]) for i in range(2)]
        relu_sq = [sb(f"relu_sq{i}", [P, GT * D]) for i in range(2)]
        turned = [sb(f"turned{i}", [P, 4 * P]) for i in range(2)]
        OUTS = 2
        wide = [sb(f"wide{i}", [P, 4 * 2 * D]) for i in range(OUTS)]
        turn_ps = [ctx.enter_context(nc.psum_tensor(f"{name}_turn_ps{i}", [P, 512], F32)) for i in range(2)]
        prod_ps = [ctx.enter_context(nc.psum_tensor(f"{name}_prod_ps{i}", [P, 2, 512], F32)) for i in range(2)]
        stats = sb("stats", [P, GT, 6])
        roots, inv_roots, newton = (sb(n, [P, 2, GT]) for n in ("roots", "inv_roots", "newton"))
        mean, var, gap, clip, arg, th, gamma, dev, inv_dev, t1 = (sb(n, [P, GT]) for n in (
            "mean", "var", "gap", "clip", "arg", "th", "gamma", "dev", "inv_dev", "t1"))

        loaded = [sem(f"loaded{i}") for i in range(2)]
        x_loaded = [sem(f"x_loaded{i}") for i in range(2)]
        tail_loaded = sem("tail_loaded")
        squared = sem("squared")
        relued = sem("relued")
        summed = sem("summed")
        tanh_in, tanh_out = sem("tanh_in"), sem("tanh_out")
        scaled = sem("scaled")
        added = sem("added")
        centred = sem("centred")
        dev_ready = sem("dev_ready")
        normed = sem("normed")
        turned_ps = sem("turned_ps")
        taken = sem("taken")
        multiplied = sem("multiplied")
        copied = sem("copied")
        kept = [sem(f"kept{i}") for i in range(2)]
        stored = [sem(f"stored{i}") for i in range(OUTS)]
        dve_chain = sem("dve_chain")
        act_chain = sem("act_chain")

        def quad(buf, k):
            return buf[:, 4 * D * k:4 * D * (k + 1)]

        def cols(buf, k):
            return buf[:, 4 * k:4 * (k + 1)]

        def group(ap, i):
            return ap[bass.ds(GT * P * i, GT * P), :].rearrange("(p t) d -> p (t d)", t=GT)

        with nc.Block() as block:

            @block.sync
            def _(sp):
                def load_sums(i, par):
                    sp.dma_start(rows[par][:, :], group(sums, i)).then_inc(loaded[par], 16)

                def load_x(i, par):
                    if isinstance(i, int) and i == NGRP - 1:
                        first = GT * P * i
                        whole, some = divmod(N - first, GT)
                        sp.dma_start(resid[par][whole:whole + 1, 0:some * D], x[first + whole * GT:N, :].rearrange(
                            "(p t) d -> p (t d)", p=1)).then_inc(tail_loaded, 16)
                        sp.wait_ge(tail_loaded, 16)
                        sp.dma_start(resid[par][0:whole, :], x[first:first + whole * GT, :].rearrange(
                            "(p t) d -> p (t d)", t=GT)).then_inc(x_loaded[par], 16)
                    else:
                        sp.dma_start(resid[par][:, :], group(x, i)).then_inc(x_loaded[par], 16)

                def step(h, par, more):
                    i = 2 * h + par
                    sp.wait_ge(added, GQ * (i + 1))
                    if more:
                        load_sums(2 * h + (2 + par), par)
                    sp.dma_start(group(x2, i), resid[par][:, :]).then_inc(kept[par], 16)
                    if more:
                        sp.wait_ge(centred, GQ * (i + 1))
                        sp.wait_ge(kept[par], 16 * (h + 1))
                        load_x(2 * h + (2 + par), par)

                for par in range(2):
                    load_sums(par, par)
                    load_x(par, par)
                with sp.Fori(0, NGRP // 2 - 2) as h:
                    for par in range(2):
                        step(h, par, True)
                for par in range(2):
                    step(NGRP // 2 - 2, par, True)
                for par in range(2):
                    step(NGRP // 2 - 1, par, False)
                for par in range(2):
                    sp.wait_ge(kept[par], 16 * (NGRP // 2))

            @block.gpsimd
            def _(pool):
                g = nc.gpsimd

                def square(h, par):
                    i = 2 * h + par
                    pool.wait_ge(loaded[par], 16 * (h + 1))
                    at_least(pool, summed, i - 1)
                    g.tensor_tensor(row_sq[par][:, :], rows[par][:, :], rows[par][:, :], ALU.mult).then_inc(squared, 1)

                def step(h, par, more):
                    i = 2 * h + par
                    pool.wait_ge(x_loaded[par], 16 * (h + 1))
                    for k in range(GQ):
                        pool.wait_ge(scaled, GQ * i + k + 1)
                        g.tensor_tensor(quad(resid[par], k), quad(resid[par], k), quad(rows[par], k), ALU.add).then_inc(added, 1)
                    if more:
                        square(h + 1, par)
                    pool.wait_ge(dev_ready, i + 1)
                    for k in range(GQ):
                        pool.wait_ge(centred, GQ * i + k + 1)
                        r = tiles(quad(fresh, k))
                        g.tensor_tensor(r, r, over(cols(inv_dev, k), D), ALU.mult).then_inc(normed, 1)

                for par in range(2):
                    square(0, par)
                for par in range(2):
                    step(0, par, True)
                with pool.Fori(1, NGRP // 2 - 1) as h:
                    for par in range(2):
                        step(h, par, True)
                for par in range(2):
                    step(NGRP // 2 - 1, par, False)

            @block.tensor
            def _(pe):
                def turn(h, par, k):
                    q = GQ * (2 * h + par) + k
                    pe.wait_ge(normed, q + 1)
                    at_least(pe, taken, q - 1)
                    for r in range(4):
                        last = pe.transpose(turn_ps[(k + par) % 2][:, r * P:(r + 1) * P],
                                            fresh[:, (4 * k + r) * D:(4 * k + r + 1) * D], c.ident[:, :])
                    last.then_inc(turned_ps, 1)

                def multiply(h, par, k):
                    q = GQ * (2 * h + par) + k
                    slot = (k + par) % 2
                    pe.wait_ge(taken, q + 1)
                    at_least(pe, copied, q - 1)
                    for r in range(4):
                        last = pe.matmul(prod_ps[slot][:, r // 2, (r % 2) * 2 * D:(r % 2 + 1) * 2 * D],
                                         turned[slot][:, r * P:(r + 1) * P], c.w_l1[:, :], start=True, stop=True)
                    last.then_inc(multiplied, 1)

                def step(h, par):
                    for k in range(GQ):
                        turn(h, par, k)
                        if k:
                            multiply(h, par, k - 1)
                    multiply(h, par, GQ - 1)

                for par in range(2):
                    step(0, par)
                with pe.Fori(1, NGRP // 2) as h:
                    for par in range(2):
                        step(h, par)

            @block.scalar
            def _(act):
                def relu(h, par, k):
                    if k == 0:
                        act.wait_ge(loaded[par], 16 * (h + 1))
                        at_least(act, summed, 2 * h + par - 1)
                    act.activation(quad(relu_sq[par], k), quad(rows[par], k), ACT.Relu).then_inc(act_chain, 1)

                def square(h, par, k):
                    q = GQ * (2 * h + par) + k
                    act.wait_ge(act_chain, q + 1)
                    act.activation(quad(relu_sq[par], k), quad(relu_sq[par], k), ACT.Square).then_inc(relued, 1)

                def relu_and_square(h, par):
                    for k in range(GQ):
                        relu(h, par, k)
                    for k in range(GQ):
                        square(h, par, k)

                def tanh(i):
                    act.wait_ge(tanh_in, i + 1)
                    act.activation(th[:, :], arg[:, :], ACT.Tanh).then_inc(tanh_out, 1)

                def take(h, par, k):
                    q = GQ * (2 * h + par) + k
                    slot = (k + par) % 2
                    act.wait_ge(turned_ps, q + 1)
                    at_least(act, multiplied, q - 1)
                    act.activation(turned[slot][:, :], turn_ps[slot][:, :], ACT.Relu).then_inc(taken, 1)

                def copy(h, par, k):
                    slot = (k + par) % 2
                    act.wait_ge(multiplied, GQ * (2 * h + par) + k + 1)
                    at_least(act, stored[slot], 16 * (GQ * h + (GQ * par + k) // 2))
                    act.activation(wide[slot][:, :].rearrange("p (a d) -> p a d", a=2), prod_ps[slot][:, :, :],
                                   ACT.Copy).then_inc(copied, 1)

                def store(i, par, k):
                    slot = (k + par) % 2
                    act.wait_ge(copied, GQ * i + k + 1)
                    act.dma_start(table[bass.ds(GT * P * i, GT * P), :].rearrange(
                        "(p t) d -> p t d", t=GT)[:, 4 * k:4 * k + 4, :].rearrange("p t d -> p (t d)"),
                        wide[slot][:, :]).then_inc(stored[slot], 16)

                def step(h, par, more):
                    i = 2 * h + par
                    for k in range(GQ):
                        take(h, par, k)
                        if more:
                            relu(h + 1, par, k)
                        if k:
                            copy(h, par, k - 1)
                            store(i, par, k - 1)
                            if more:
                                square(h + 1, par, k - 1)
                        if k == 1 and (more or par == 0):
                            tanh(i + 1)
                    copy(h, par, GQ - 1)
                    store(i, par, GQ - 1)
                    if more:
                        square(h + 1, par, GQ - 1)

                relu_and_square(0, 0)
                tanh(0)
                relu_and_square(0, 1)
                for par in range(2):
                    step(0, par, True)
                with act.Fori(1, NGRP // 2 - 1) as h:
                    for par in range(2):
                        step(h, par, True)
                for par in range(2):
                    step(NGRP // 2 - 1, par, False)
                for k in range(OUTS):
                    act.wait_ge(stored[k], 16 * (NQ // OUTS))

            @block.vector
            def _(dve):
                v = nc.vector
                S, R = roots[:, 0, :], roots[:, 1, :]
                inv_s, inv_r = inv_roots[:, 0, :], inv_roots[:, 1, :]

                def gammas(h, par, link):
                    i = 2 * h + par
                    dve.wait_ge(squared, i + 1)
                    v.tensor_reduce(S, tiles(row_sq[par][:, :]), X, ALU.add)
                    dve.wait_ge(relued, GQ * (i + 1))
                    link(v.tensor_reduce(R, tiles(relu_sq[par][:, :]), X, ALU.add))
                    dve.sem_inc(summed, 1)
                    link(v.tensor_scalar(roots[:, :, :], roots[:, :, :], TINY, None, ALU.max))
                    inverse_root(v, link, inv_roots[:, :, :], roots[:, :, :], newton[:, :, :])
                    v.tensor_scalar(clip[:, :], inv_s, ATANH_MAX, 1.0, ALU.mult, ALU.min)
                    link(v.tensor_tensor(arg[:, :], R, inv_r, ALU.mult))
                    link(v.tensor_tensor(arg[:, :], arg[:, :], clip[:, :], ALU.mult))
                    dve.sem_inc(tanh_in, 1)

                def step(h, par, link, more):
                    i = 2 * h + par
                    dve.wait_ge(tanh_out, i + 1)
                    link(v.scalar_tensor_tensor(out=gamma[:, :], in0=th[:, :], scalar=BALL, in1=inv_r, op0=ALU.min, op1=ALU.mult))
                    for k in range(GQ):
                        r = tiles(quad(rows[par], k))
                        v.scalar_tensor_tensor(out=r, in0=r, scalar=0.0, in1=over(cols(gamma, k), D),
                                               op0=ALU.max, op1=ALU.mult).then_inc(scaled, 1)
                    res = tiles(resid[par][:, :])

                    def stats_of(t):
                        if t % 4 == 0:
                            dve.wait_ge(added, GQ * i + t // 4 + 1)
                        return v.bn_stats(stats[:, t, :], res[:, t, :])

                    for t in range(GT):
                        last = stats_of(t)
                    link(last)
                    v.tensor_tensor(gap[:, :], stats[:, :, 1], stats[:, :, 4], ALU.subtract)
                    v.tensor_tensor(var[:, :], stats[:, :, 2], stats[:, :, 5], ALU.add)
                    link(v.tensor_tensor(mean[:, :], stats[:, :, 1], stats[:, :, 4], ALU.add))
                    v.tensor_scalar(mean[:, :], mean[:, :], 0.5, None, ALU.mult)
                    v.tensor_scalar(var[:, :], var[:, :], 1.0 / D, 1e-5, ALU.mult, ALU.add)
                    link(v.tensor_tensor(gap[:, :], gap[:, :], gap[:, :], ALU.mult))
                    link(v.scalar_tensor_tensor(out=dev[:, :], in0=gap[:, :], scalar=0.25, in1=var[:, :],
                                                op0=ALU.mult, op1=ALU.add))
                    at_least(dve, normed, GQ * i)

                    def centre(k):
                        at_least(dve, turned_ps, GQ * (i - 1) + k + 1)
                        v.tensor_tensor(tiles(quad(fresh, k)), res[:, 4 * k:4 * k + 4, :],
                                        over(cols(mean, k), D), ALU.subtract).then_inc(centred, 1)

                    link.beside(lambda n: centre(n) if n < GQ else None)
                    inverse_root(v, link, inv_dev[:, :], dev[:, :], t1[:, :])
                    dve.sem_inc(dev_ready, 1)
                    link.beside(None)
                    if more:
                        gammas(h + par, 1 - par, link)

                before = 14
                link = Chain(dve, dve_chain, 0)
                gammas(0, 0, link)
                assert link.count == before, link.count
                for par in range(2):
                    step(0, par, Chain(dve, dve_chain, before + par * RESIDUAL_LINKS), True)
                with dve.Fori(1, NGRP // 2 - 1) as h:
                    for par in range(2):
                        step(h, par, Chain(dve, dve_chain, before + (2 * h + par) * RESIDUAL_LINKS), True)
                for par in range(2):
                    link = Chain(dve, dve_chain, before + (NGRP - 2 + par) * RESIDUAL_LINKS)
                    step(NGRP // 2 - 1, par, link, par == 0)
                    if par == 0:
                        assert link.count == before + (NGRP - 1) * RESIDUAL_LINKS, link.count - before - (NGRP - 2) * RESIDUAL_LINKS



def edge_pass(nc, c, name, table, dst_rows, sums, out=None, x2=None):
    last = out is not None
    width = 2 * D if last else D
    with semaphores(nc, name) as sem, ExitStack() as ctx:
        def sb(n, shape, dtype=F32):
            return ctx.enter_context(nc.sbuf_tensor(f"{name}_{n}", shape, dtype))

        BANKS = RING // 2
        ring = sb("ring", [P, RING * 4 * width])
        index = sb("index", [P, RING * 4], I32)
        select = [sb(f"select{i}", [P, 4 * PAIRS, P]) for i in range(2)]
        stage = [sb(f"stage{i}", [P, 4 * D]) for i in range(BANKS)]
        sum_ps = [ctx.enter_context(nc.psum_tensor(f"{name}_sum_ps{i}", [P, 512], F32)) for i in range(BANKS)]

        landed = [sem(f"landed{i}") for i in range(RING)]
        may_gather = sem("may_gather")
        indexed = sem("indexed")
        weighed = sem("weighed")
        messages = sem("messages")
        selected = sem("selected")
        added = sem("added")
        taken = sem("taken")
        x2_in = [sem(f"x2_in{i}") for i in range(BANKS)] if last else None
        stored = [sem(f"stored{i}") for i in range(BANKS)]
        dve_chain = sem("dve_chain")

        groups = -(-NQ // RING)
        spare = 9

        def over_groups(eng, step):
            def body(g):
                for k in range(RING):
                    if not (isinstance(g, int) and RING * g + k >= NQ):
                        step(g, k)
            body(0)
            with eng.Fori(1, groups - 1) as g:
                body(g)
            body(groups - 1)

        def exists(q):
            return not (isinstance(q, int) and q >= NQ)

        def wait_landed(eng, g, k):
            g, k = (g, k) if k < RING else (g + 1, k - RING)
            short = isinstance(g, int) and RING * g + k == NQ - 1
            eng.wait_ge(landed[k], 64 * (g + 1) - (16 * (4 * NQ - ET) if short else 0))

        def ring_quad(k):
            return ring[:, (k % RING) * 4 * width:(k % RING + 1) * 4 * width].rearrange("p (t d) -> p t d", d=width)

        def node_rows(ap, q):
            return ap[bass.ds(4 * P * q, 4 * P), :].rearrange("(t p) d -> p t d", p=P)


        def fast_pool(pool):
            def step(g, k):
                q = RING * g + k
                pool.wait_ge(indexed, q + 1)
                if not (isinstance(g, int) and g == 0):
                    pool.wait_ge(added, q - RING + AHEAD + 1)
                pool.sem_inc(may_gather, 1)
                for t in range(4):
                    if isinstance(g, int) and 4 * q + t >= ET:
                        break
                    at = 4 * k + t
                    nc.gpsimd.indirect_dma_start(
                        out=ring[:, at * width:(at + 1) * width], out_offset=None, in_=table,
                        in_offset=bass.IndirectOffsetOnAxis(ap=index[:, at:at + 1].bitcast(U32), axis=0)).then_inc(landed[k], 16)

            over_groups(pool, step)

        def fast_pe(pe):
            slots = c.slot_row_wide if last else c.slot_row

            def load(numbers):
                return nc.values_load_multi_w_load_instructions(
                    numbers, engines=(mybir.EngineType.PE,), min_val=0, max_val=(4 * RING - 1) * width,
                    skip_runtime_bounds_check_because="the tables pass made the ring slots, each less its whole laps")[1]

            def step(g, k):
                q = RING * g + k
                numbers = load(slots[0:1, bass.ds(q, 1), 0:9])
                use_third = numbers[8]
                if isinstance(q, int):
                    pe.wait_ge(messages, min(q + AHEAD + 1, NQ))
                else:
                    pe.wait_ge(messages, q + AHEAD + 1)
                pe.wait_ge(selected, q + 1)
                at_least(pe, taken, q - BANKS + 1)

                def pair(r, j, where, **flags):
                    return pe.matmul(sum_ps[k % BANKS][:, r * D:(r + 1) * D], select[k % 2][:, PAIRS * r + j, :],
                                     ring[:, bass.ds(where, D)], **flags)

                pe.matmul(sum_ps[k % BANKS][:, :], c.zero_row[0:1, 0:P], c.zero_row[0:1, :], start=True, stop=False)
                with pe.If(use_third > 0):
                    third = load(slots[0:1, bass.ds(q, 1), 9:13])
                    for r in range(4):
                        pair(r, 2, third[r], start=False, stop=False)
                for r in range(4):
                    for j in range(2):
                        mm = pair(r, j, numbers[2 * r + j], start=False, stop=r == 3 and j == 1)
                mm.then_inc(added, 1)

            over_groups(pe, step)

        def fast_act(act):
            def fill_index(q, k):
                src = c.src_col[:, bass.ds(4 * q, 4)]
                act.activation(index[:, 4 * (k % RING):4 * (k % RING) + 4], src, ACT.Copy).then_inc(indexed, 1)

            def weigh(g, k):
                q = RING * g + k
                wait_landed(act, g, k)
                for t in range(4):
                    half = ring_quad(k)[:, t, D:2 * D]
                    ins = act.activation(half, half, ACT.Copy, scale=c.attr_col[1][:, bass.ds(4 * q + t, 1)])
                ins.then_inc(weighed, 1)

            def step(g, k):
                q = RING * g + k
                if last:
                    if exists(q + AHEAD):
                        weigh(g, k + AHEAD)
                else:
                    act.wait_ge(added, q + 1)
                    at_least(act, stored[k % BANKS], 16 * (2 * g + k // BANKS))
                    act.activation(stage[k % BANKS][:, :], sum_ps[k % BANKS][:, :], ACT.Copy).then_inc(taken, 1)
                if exists(q + spare):
                    fill_index(q + spare, k + spare)

            for q in range(spare):
                fill_index(q, q)
            if last:
                for q in range(AHEAD):
                    weigh(0, q)
            over_groups(act, step)

        def fast_dve(dve):
            v = nc.vector

            def message(g, k, q):
                wait_landed(dve, g, k)
                m = ring_quad(k)[:, :, 0:D]
                if last:
                    v.tensor_tensor(m, m, over(c.attr_col[0][:, bass.ds(4 * q, 4)], D), ALU.mult).then_inc(dve_chain, 1)
                else:
                    v.tensor_tensor(m, m, over(c.weight_col[:, bass.ds(4 * q, 4)], D), ALU.mult).then_inc(messages, 1)

            def message_rest(k, q):
                m = ring_quad(k)[:, :, 0:D]
                dve.wait_ge(weighed, q + 1)
                dve.wait_ge(dve_chain, 2 * q + 1)
                v.tensor_tensor(m, m, ring_quad(k)[:, :, D:2 * D], ALU.add).then_inc(dve_chain, 1)
                dve.wait_ge(dve_chain, 2 * q + 2)
                v.tensor_tensor(m, m, under(c.b_l1[:, :], 4), ALU.add).then_inc(messages, 1)

            def finish(g, k, q):
                dve.wait_ge(added, q + 1)
                dve.wait_ge(x2_in[k % BANKS], 32 * (2 * g + k // BANKS + 1))
                v.tensor_tensor(stage[k % BANKS][:, :], stage[k % BANKS][:, :], sum_ps[k % BANKS][:, :], ALU.add).then_inc(taken, 1)

            def step(g, k):
                q = RING * g + k
                if exists(q + AHEAD):
                    message(g, k + AHEAD, q + AHEAD)
                at_least(dve, added, q - 1)
                rel = c.dst_in_tile[:, bass.ds(4 * q, 4), :].rearrange("p t j -> p (t j)")
                v.tensor_tensor(select[k % 2][:, :, :], under(c.iota_row[:, :], 4 * PAIRS), over(rel, P),
                                ALU.is_equal).then_inc(selected, 1)
                if last:
                    if exists(q + AHEAD):
                        message_rest(k + AHEAD, q + AHEAD)
                    if not (isinstance(q, int) and q == 0):
                        finish(*((g, k - 1) if k else (g - 1, RING - 1)), q - 1)

            for q in range(AHEAD):
                message(0, q, q)
                if last:
                    message_rest(q, q)
            over_groups(dve, step)
            if last:
                finish(groups - 1, (NQ - 1) % RING, NQ - 1)

        def fast_sp(sp):
            def load_x2(g, k, q):
                slot = k % BANKS
                if not (isinstance(q, int) and q < BANKS):
                    sp.wait_ge(stored[slot], 16 * (2 * g + (k // BANKS)))
                for half in range(2):
                    part = slice(64 * half, 64 * half + 64)
                    sp.dma_start(tiles(stage[slot][:, :])[part], node_rows(x2, q)[part]).then_inc(x2_in[slot], 16)

            def step(g, k):
                q = RING * g + k
                slot = k % BANKS
                if last:
                    if exists(q + 3):
                        load_x2(*((g, k + 3) if k + 3 < RING else (g + 1, k + 3 - RING)), q + 3)
                sp.wait_ge(taken, q + 1)
                if last and isinstance(q, int) and q == NQ - 1:
                    whole = NT - 1 - 4 * q
                    first = 4 * P * q
                    sp.dma_start(out[first:first + whole * P, :].rearrange("(t p) d -> p t d", p=P),
                                 tiles(stage[slot][:, :])[:, 0:whole, :]).then_inc(stored[slot], 16)
                    sp.dma_start(out[first + whole * P:N, :],
                                 stage[slot][0:TAIL, whole * D:(whole + 1) * D]).then_inc(stored[slot], 16)
                else:
                    sp.dma_start(node_rows(out if last else sums, q), tiles(stage[slot][:, :])).then_inc(stored[slot], 16)

            if last:
                for q in range(3):
                    load_x2(0, q, q)
            over_groups(sp, step)
            for slot in range(BANKS):
                uses = len(range(slot, NQ, BANKS)) + (1 if last and (NQ - 1) % BANKS == slot else 0)
                sp.wait_ge(stored[slot], 16 * uses)

        s_index, s_target = sb("s_index", [P, 1], I32), sb("s_target", [P, 1], I32)
        s_rows, s_message = sb("s_rows", [P, D]), sb("s_message", [P, width])
        s_dst, s_same, s_before = sb("s_dst", [P, P]), sb("s_same", [P, P]), sb("s_before", [P, P])
        s_first, s_real, s_goal = sb("s_first", [P, 1]), sb("s_real", [P, 1]), sb("s_goal", [P, 1])
        s_zeroed = sem("s_zeroed")
        s_indexed = sem("s_indexed")
        s_gathered = sem("s_gathered")
        s_dst_in = sem("s_dst_in")
        s_targeted = sem("s_targeted")
        s_ready = sem("s_ready")
        s_summed = sem("s_summed")
        s_fetched = sem("s_fetched")
        s_added = sem("s_added")
        s_written = sem("s_written")
        s_chain = sem("s_chain")
        OUT_P, OUT_T = 125, 4
        chunks = N // (OUT_P * OUT_T)

        def over_tiles(eng, step, n):
            step(0)
            with eng.Fori(1, n) as e:
                step(e)

        def slow_sp(sp):
            def zero(q):
                sp.dma_start(sums[bass.ds(4 * P * q, 4 * P), :].rearrange("(p t) d -> p (t d)", t=4), c.zeros[:, :]).then_inc(s_zeroed, 16)

            with sp.Fori(0, NQ) as q:
                zero(q)
            sp.dma_start(sums[ROWS:ROWS + P, :], c.zeros[:, 0:D]).then_inc(s_zeroed, 16)

            def step(e):
                at_least(sp, s_written, 16 * e)
                sp.dma_start(s_dst[:, :], dst_rows[bass.ds(e, 1), :].broadcast_to([P, P])).then_inc(s_dst_in, 16)

            over_tiles(sp, step, ET)
            sp.wait_ge(s_written, 16 * ET)
            if last:
                def chunk(ap, n):
                    return ap[bass.ds(OUT_P * OUT_T * n, OUT_P * OUT_T), :].rearrange("(p t) d -> p (t d)", t=OUT_T)

                def finish(n):
                    at_least(sp, stored[0], 16 * n)
                    sp.dma_start(stage[0][0:OUT_P, :], chunk(sums, n)).then_inc(x2_in[0], 16)
                    sp.dma_start(stage[1][0:OUT_P, :], chunk(x2, n)).then_inc(x2_in[0], 16)
                    sp.wait_ge(taken, n + 1)
                    sp.dma_start(chunk(out, n), stage[0][0:OUT_P, :]).then_inc(stored[0], 16)

                over_tiles(sp, finish, chunks)
                sp.wait_ge(stored[0], 16 * chunks)

        def slow_pool(pool):
            def step(e):
                pool.wait_ge(s_indexed, e + 1)
                pool.sem_inc(may_gather, 1)
                nc.gpsimd.indirect_dma_start(out=s_message[:, :], out_offset=None, in_=table, in_offset=bass.IndirectOffsetOnAxis(
                    ap=s_index[:, 0:1].bitcast(U32), axis=0)).then_inc(s_gathered, 16)
                pool.wait_ge(s_targeted, e + 1)
                if isinstance(e, int) and e == 0:
                    pool.wait_ge(s_zeroed, 16 * (NQ + 1))
                pool.sem_inc(may_gather, 1)
                nc.gpsimd.indirect_dma_start(out=s_rows[:, :], out_offset=None, in_=sums, in_offset=bass.IndirectOffsetOnAxis(
                    ap=s_target[:, 0:1].bitcast(U32), axis=0)).then_inc(s_fetched, 16)
                pool.wait_ge(s_added, e + 1)
                pool.sem_inc(may_gather, 1)
                nc.gpsimd.indirect_dma_start(out=sums, out_offset=bass.IndirectOffsetOnAxis(
                    ap=s_target[:, 0:1].bitcast(U32), axis=0), in_=s_rows[:, :], in_offset=None).then_inc(s_written, 16)
                pool.wait_ge(s_written, 16 * (e + 1))

            over_tiles(pool, step, ET)

        def slow_pe(pe):
            def step(e):
                pe.wait_ge(s_ready, e + 1)
                pe.matmul(sum_ps[0][:, 0:D], s_same[:, :], s_message[:, 0:D], start=True, stop=True).then_inc(s_summed, 1)

            over_tiles(pe, step, ET)

        def slow_dve(dve):
            v = nc.vector
            links = 5 + (3 if last else 1)

            def step(e):
                link = Chain(dve, s_chain, links * e)
                dst = c.dst_col[:, bass.ds(e, 1)]
                at_least(dve, s_written, 16 * e)
                v.tensor_copy(s_index[:, :], c.src_col[:, bass.ds(e, 1)]).then_inc(s_indexed, 1)
                dve.wait_ge(s_dst_in, 16 * (e + 1))
                v.tensor_scalar(s_real[:, :], dst, float(N), None, ALU.is_lt)
                v.tensor_tensor(s_goal[:, :], dst, c.trash[:, :], ALU.subtract)
                link(v.tensor_scalar(s_same[:, :], s_dst[:, :], dst, None, ALU.is_equal))
                link(v.tensor_tensor(s_before[:, :], s_same[:, :], c.earlier[:, :], ALU.mult))
                link(v.tensor_reduce(s_first[:, :], s_before[:, :], X, ALU.add))
                link(v.scalar_tensor_tensor(out=s_first[:, :], in0=s_first[:, :], scalar=0.0, in1=s_real[:, :],
                                            op0=ALU.is_equal, op1=ALU.mult))
                link(v.scalar_tensor_tensor(out=s_goal[:, :], in0=s_goal[:, :], scalar=s_first[:, 0:1], in1=c.trash[:, :],
                                            op0=ALU.mult, op1=ALU.add))
                v.tensor_copy(s_target[:, :], s_goal[:, :]).then_inc(s_targeted, 1)
                dve.wait_ge(s_gathered, 16 * (e + 1))
                m = s_message[:, 0:D]
                if last:
                    link(v.tensor_scalar(m, m, c.attr_col[0][:, bass.ds(e, 1)], None, ALU.mult))
                    link(v.scalar_tensor_tensor(out=m, in0=s_message[:, D:2 * D], scalar=c.attr_col[1][:, bass.ds(e, 1)], in1=m,
                                                op0=ALU.mult, op1=ALU.add))
                    link(v.tensor_tensor(m, m, c.b_l1[:, :], ALU.add))
                else:
                    link(v.tensor_scalar(m, m, c.weight_col[:, bass.ds(e, 1)], None, ALU.mult))
                dve.sem_inc(s_ready, 1)
                dve.wait_ge(s_summed, e + 1)
                dve.wait_ge(s_fetched, 16 * (e + 1))
                v.tensor_tensor(s_rows[:, :], s_rows[:, :], sum_ps[0][:, 0:D], ALU.add).then_inc(s_added, 1)

            over_tiles(dve, step, ET)
            if last:
                def finish(n):
                    dve.wait_ge(x2_in[0], 32 * (n + 1))
                    v.tensor_tensor(stage[0][0:OUT_P, :], stage[0][0:OUT_P, :], stage[1][0:OUT_P, :], ALU.add).then_inc(taken, 1)

                over_tiles(dve, finish, chunks)

        def either(eng, slow, fast):
            is_slow = eng.value_load(c.slow[0:1, 0:1], min_val=0, max_val=1)
            with eng.If(is_slow > 0):
                slow(eng)
            with eng.Else():
                fast(eng)

        with nc.Block() as block:

            @block.sync
            def _(sp):
                either(sp, slow_sp, fast_sp)

            @block.gpsimd
            def _(pool):
                either(pool, slow_pool, fast_pool)

            @block.tensor
            def _(pe):
                either(pe, slow_pe, fast_pe)

            @block.vector
            def _(dve):
                either(dve, slow_dve, fast_dve)

            @block.scalar
            def _(act):
                is_slow = act.value_load(c.slow[0:1, 0:1], min_val=0, max_val=1)
                with act.If(is_slow < 1):
                    fast_act(act)


def build(nc, x, src, dst, edge_attr_2, edge_weight, W1, b1, W2, b2, W, b, out):
    with ExitStack() as ctx:
        def scratch(name, shape):
            return nc.dram_tensor(name, shape, F32, kind="Internal").ap()

        c = Constants(lambda n, s, d: ctx.enter_context(nc.sbuf_tensor(n, s, d)))
        io = dict(x=x, src=src, dst=dst, edge_attr_2=edge_attr_2, edge_weight=edge_weight, W1=W1, b1=b1, W2=W2, b2=b2, W=W, b=b)
        dram = dict(dst_rows=scratch("dst_rows", (COLS, P)), slots=scratch("slots", (2, COLS * 4)))
        table = scratch("table", (ROWS, D))
        sums = scratch("sums", (ROWS + P, D))
        x2 = scratch("x2", (ROWS, D))
        wide = scratch("wide", (ROWS, 2 * D))
        tables_pass(nc, c, io, dram)
        hyper_pass(nc, c, "la", 0, x, table, True)
        edge_pass(nc, c, "ea", table, dram["dst_rows"], sums)
        hyper_pass(nc, c, "lb", 1, sums, table, False)
        edge_pass(nc, c, "eb", table, dram["dst_rows"], sums)
        residual_pass(nc, c, "rs", sums, x, x2, wide)
        edge_pass(nc, c, "ec", wide, dram["dst_rows"], sums, out, x2)


_INS = ["x", "src", "dst", "edge_attr_2", "edge_weight", "L0_gnn_W1", "L0_gnn_b1", "L0_gnn_W2", "L0_gnn_b2", "L1_gnn_W", "L1_gnn_b"]


def kernel(**inputs):
    import numpy as _np
    import concourse.bacc as _bacc
    from concourse import mybir as _mybir
    from concourse.bass_utils import run_bass_kernel_spmd as _run

    nc = _bacc.Bacc("TRN2", target_bir_lowering=False, num_devices=1)
    arrays, args = {}, []
    for name in _INS:
        a = _np.ascontiguousarray(inputs[name])
        arrays[f"in_{name}"] = a
        args.append(nc.dram_tensor(f"in_{name}", a.shape, _mybir.dt.from_np(a.dtype), kind="ExternalInput").ap())
    args.append(nc.dram_tensor("out_0", (N, D), F32, kind="ExternalOutput").ap())
    build(nc, *args)
    return _run(nc, [arrays], core_ids=[0]).results[0]["out_0"]
```
